# Optimizing a Trainium2 kernel written in Bass

```python
import numpy as np
import jax
import jax.numpy as jnp

def _softmax(x, axis=-1):
    return jax.nn.softmax(x, axis=axis)

def _gelu(x):
    return jax.nn.gelu(x, approximate=True)

def _silu(x):
    return jax.nn.silu(x)

def _sigmoid(x):
    return jax.nn.sigmoid(x)

def _layernorm(x, axis=-1, eps=1e-05):
    m = jnp.mean(x, axis=axis, keepdims=True)
    v = jnp.var(x, axis=axis, keepdims=True)
    return (x - m) / jnp.sqrt(v + eps)

def _scatter_add(tgt, idx, src, axis=0):
    return tgt.at[idx].add(src)

def _segment_sum(src, seg, n):
    return jax.ops.segment_sum(src, seg, n)
kernel_name = 'mk_seq_preln_d1_jaxref_r8_0c1830'

def setup_inputs(seed: int=0):
    np.random.seed(seed)
    _w = jnp.asarray

    def _L0_attn_setup():
        import jax, jax.numpy as jnp
        import numpy as np
        D, B, L, E, H, F = (6, 4, 256, 128, 16, 512)
        DH = E // H
        DECAY = 16.0
        CSCALE = 1.0
        EPS = 1e-05

        def _ln(x, w, b):
            m = jnp.mean(x, axis=-1, keepdims=True)
            v = jnp.mean(jnp.square(x - m), axis=-1, keepdims=True)
            return (x - m) * jax.lax.rsqrt(v + EPS) * w + b
        key = jax.random.key(seed)
        ks = jax.random.split(key, 10)
        s = 0.02
        f32 = jnp.float32
        return {'x': jax.random.normal(ks[0], (B, L, E), f32), 'Wq': jax.random.normal(ks[1], (D, E, E), f32) * s, 'Wk': jax.random.normal(ks[2], (D, E, E), f32) * s, 'bq': jnp.zeros((D, E), f32), 'bk': jnp.zeros((D, E), f32), 'ln1_w': jnp.ones((D, E), f32), 'ln1_b': jnp.zeros((D, E), f32), 'ln2_w': jnp.ones((D, E), f32), 'ln2_b': jnp.zeros((D, E), f32), 'ln3_w': jnp.ones((D, E), f32), 'ln3_b': jnp.zeros((D, E), f32), 'W1': jax.random.normal(ks[3], (D, F, E), f32) * s, 'b1': jnp.zeros((D, F), f32), 'W2': jax.random.normal(ks[4], (D, E, F), f32) * s, 'b2': jnp.zeros((D, E), f32)}
    _L0_attn_in = _L0_attn_setup()

    def _L0_ffn_setup():
        import jax, jax.numpy as jnp
        import numpy as np
        D_IN, D_HID = (128, 512)

        def _ternary(key, shape):
            return jax.random.randint(key, shape, -1, 2).astype(jnp.float32)

        def _tlin(x, w, s):
            return jnp.einsum('bsi,oi->bso', x, w) * s
        key = jax.random.key(seed)
        ks = jax.random.split(key, 12)
        inv = lambda fan: 1.0 / np.sqrt(fan).astype(np.float32)
        return {'x': jax.random.normal(ks[0], (4, 256, D_IN), dtype=jnp.float32), 'w1_w': _ternary(ks[1], (D_HID, D_IN)), 'w1_s': jax.random.uniform(ks[2], (D_HID,), dtype=jnp.float32) * inv(D_IN), 'w2_w': _ternary(ks[3], (D_HID, D_IN)), 'w2_s': jax.random.uniform(ks[4], (D_HID,), dtype=jnp.float32) * inv(D_IN), 'h1_w': _ternary(ks[5], (D_HID, D_HID)), 'h1_s': jax.random.uniform(ks[6], (D_HID,), dtype=jnp.float32) * inv(D_HID), 'h2_w': _ternary(ks[7], (D_HID, D_HID)), 'h2_s': jax.random.uniform(ks[8], (D_HID,), dtype=jnp.float32) * inv(D_HID), 'w3_w': _ternary(ks[9], (D_IN, D_HID)), 'w3_s': jax.random.uniform(ks[10], (D_IN,), dtype=jnp.float32) * inv(D_HID)}
    _L0_ffn_in = _L0_ffn_setup()
    _d = {'L0_attn_x': _L0_attn_in['x'], 'L0_attn_Wq': _L0_attn_in['Wq'], 'L0_attn_Wk': _L0_attn_in['Wk'], 'L0_attn_bq': _L0_attn_in['bq'], 'L0_attn_bk': _L0_attn_in['bk'], 'L0_attn_ln1_w': _L0_attn_in['ln1_w'], 'L0_attn_ln1_b': _L0_attn_in['ln1_b'], 'L0_attn_ln2_w': _L0_attn_in['ln2_w'], 'L0_attn_ln2_b': _L0_attn_in['ln2_b'], 'L0_attn_ln3_w': _L0_attn_in['ln3_w'], 'L0_attn_ln3_b': _L0_attn_in['ln3_b'], 'L0_attn_W1': _L0_attn_in['W1'], 'L0_attn_b1': _L0_attn_in['b1'], 'L0_attn_W2': _L0_attn_in['W2'], 'L0_attn_b2': _L0_attn_in['b2'], 'L0_ffn_w1_w': _L0_ffn_in['w1_w'], 'L0_ffn_w1_s': _L0_ffn_in['w1_s'], 'L0_ffn_w2_w': _L0_ffn_in['w2_w'], 'L0_ffn_w2_s': _L0_ffn_in['w2_s'], 'L0_ffn_h1_w': _L0_ffn_in['h1_w'], 'L0_ffn_h1_s': _L0_ffn_in['h1_s'], 'L0_ffn_h2_w': _L0_ffn_in['h2_w'], 'L0_ffn_h2_s': _L0_ffn_in['h2_s'], 'L0_ffn_w3_w': _L0_ffn_in['w3_w'], 'L0_ffn_w3_s': _L0_ffn_in['w3_s']}
    _x0 = _d['L0_attn_x']
    _d['L0_attn_x'] = jax.random.normal(jax.random.fold_in(jax.random.key(seed), 1), (8, 512, 128), dtype=_x0.dtype)
    del _x0
    return _d

def reference(L0_attn_x, L0_attn_Wq, L0_attn_Wk, L0_attn_bq, L0_attn_bk, L0_attn_ln1_w, L0_attn_ln1_b, L0_attn_ln2_w, L0_attn_ln2_b, L0_attn_ln3_w, L0_attn_ln3_b, L0_attn_W1, L0_attn_b1, L0_attn_W2, L0_attn_b2, L0_ffn_w1_w, L0_ffn_w1_s, L0_ffn_w2_w, L0_ffn_w2_s, L0_ffn_h1_w, L0_ffn_h1_s, L0_ffn_h2_w, L0_ffn_h2_s, L0_ffn_w3_w, L0_ffn_w3_s):

    def _L0_attn_ref(x, Wq, Wk, bq, bk, ln1_w, ln1_b, ln2_w, ln2_b, ln3_w, ln3_b, W1, b1, W2, b2):
        import jax, jax.numpy as jnp
        import numpy as np
        D, B, L, E, H, F = (6, 4, 256, 128, 16, 512)
        DH = E // H
        DECAY = 16.0
        CSCALE = 1.0
        EPS = 1e-05

        def _ln(x, w, b):
            m = jnp.mean(x, axis=-1, keepdims=True)
            v = jnp.mean(jnp.square(x - m), axis=-1, keepdims=True)
            return (x - m) * jax.lax.rsqrt(v + EPS) * w + b
        seq = x.shape[1]
        pos = jnp.arange(seq)
        rel = jnp.exp(-jnp.abs(pos[:, None] - pos[None, :]).astype(x.dtype) / DECAY)
        inv_sqrt_d = 1.0 / np.sqrt(DH)

        def layer(h, p):
            wq, wk, bq_, bk_, l1w, l1b, l2w, l2b, l3w, l3b, w1, b1_, w2, b2_ = p
            bh, sl, _ = h.shape
            q = (h @ wq.T + bq_).reshape(bh, sl, H, DH)
            k = (h @ wk.T + bk_).reshape(bh, sl, H, DH)
            scores = jnp.einsum('blhd,bmhd->bhlm', q, k) * inv_sqrt_d
            w_avg = jax.nn.softmax(scores, axis=-1).mean(axis=1)
            new_w = jax.nn.softmax(CSCALE * w_avg + rel[None], axis=-1)
            sa = jnp.einsum('blm,bme->ble', new_w, h)
            h1 = _ln(h + sa, l1w, l1b)
            h2 = _ln(h1, l2w, l2b)
            ff = jax.nn.relu(h2 @ w1.T + b1_) @ w2.T + b2_
            return (_ln(h2 + ff, l3w, l3b), None)
        out, _ = jax.lax.scan(layer, x, (Wq, Wk, bq, bk, ln1_w, ln1_b, ln2_w, ln2_b, ln3_w, ln3_b, W1, b1, W2, b2))
        return out

    def _L0_ffn_ref(x, w1_w, w1_s, w2_w, w2_s, h1_w, h1_s, h2_w, h2_s, w3_w, w3_s):
        import jax, jax.numpy as jnp
        import numpy as np
        D_IN, D_HID = (128, 512)

        def _ternary(key, shape):
            return jax.random.randint(key, shape, -1, 2).astype(jnp.float32)

        def _tlin(x, w, s):
            return jnp.einsum('bsi,oi->bso', x, w) * s
        h = jax.nn.silu(_tlin(x, w1_w, w1_s)) * _tlin(x, w2_w, w2_s)
        h = jax.nn.gelu(_tlin(h, h1_w, h1_s), approximate=False)
        h = jax.nn.gelu(_tlin(h, h2_w, h2_s), approximate=False)
        return _tlin(h, w3_w, w3_s)
    x = L0_attn_x
    x = x + _L0_attn_ref(_layernorm(x, axis=-1), L0_attn_Wq, L0_attn_Wk, L0_attn_bq, L0_attn_bk, L0_attn_ln1_w, L0_attn_ln1_b, L0_attn_ln2_w, L0_attn_ln2_b, L0_attn_ln3_w, L0_attn_ln3_b, L0_attn_W1, L0_attn_b1, L0_attn_W2, L0_attn_b2)
    x = x + _L0_ffn_ref(_layernorm(x, axis=-1), L0_ffn_w1_w, L0_ffn_w1_s, L0_ffn_w2_w, L0_ffn_w2_s, L0_ffn_h1_w, L0_ffn_h1_s, L0_ffn_h2_w, L0_ffn_h2_s, L0_ffn_w3_w, L0_ffn_w3_s)
    return x

_drawn_inputs = setup_inputs


def setup_inputs(seed=0):
    import zlib

    import numpy as np

    out = dict(_drawn_inputs(seed))
    spreads = {'L0_attn_bq': (0.0, 0.1),
     'L0_attn_bk': (0.0, 0.1),
     'L0_attn_ln1_w': (1.0, 0.2),
     'L0_attn_ln1_b': (0.0, 0.1),
     'L0_attn_ln2_w': (1.0, 0.2),
     'L0_attn_ln2_b': (0.0, 0.1),
     'L0_attn_ln3_w': (1.0, 0.2),
     'L0_attn_ln3_b': (0.0, 0.1),
     'L0_attn_b1': (0.0, 0.1),
     'L0_attn_b2': (0.0, 0.1)}
    factors = {}
    for name, (base, spread) in spreads.items():
        noise = np.random.default_rng([zlib.crc32(name.encode()), seed]).standard_normal(out[name].shape)
        drawn = base * np.exp(spread * noise) if base else spread * noise
        out[name] = jnp.asarray(drawn.astype(out[name].dtype))
    for name, factor in factors.items():
        out[name] = (out[name] * factor).astype(out[name].dtype)
    return out
```

```python
import concourse.bass as bass
from concourse import mybir
from contextlib import ExitStack

D, B, S, E, H, F = 6, 8, 512, 128, 16, 512
DH = E // H
P = 128
NT = S // P
NG = 4
HG = H // NG
QS = P // HG
NQ = NT * NG
TILES = NQ * 4
U = D * B
CH = F // P
EPS = 1e-5
NS = 5
ET = 16
LOADS = 3 + 3 * HG
C_B1, C_B2, C_W2, C_BB2, C_W3, C_BB3 = 0, 4, 5, 6, 7, 8
NCOL = 9


def build(nc, x, wqk, bqk, w1t, w2t, cols, rows, fw1, fw2, fh1, fh2, fw3, fcols, frow, gmat, sel, ident, out):
    f32, f32r = mybir.dt.float32, mybir.dt.float32r
    ALU, ACT, AX = mybir.AluOpType, mybir.ActivationFunctionType, mybir.AxisListType.X
    ctx = ExitStack()
    with ctx:
        def sb(name, shape, dt=f32):
            return ctx.enter_context(nc.sbuf_tensor(name, shape, dt))

        def sem(name):
            return ctx.enter_context(nc.semaphore(name))

        qk_dram = nc.dram_tensor("qk_split", [B, 4, P, S], f32, kind="Internal").ap()

        y_dram = nc.dram_tensor("y_kept", [B, P, NT, E], f32, kind="Internal").ap()

        hc = [sb(f"hc{i}", [P, NT, E + 1]) for i in range(2)]
        hs = sb("hs", [P, B, NT, E])
        ex = sb("ex", [P, ET, S])
        negmax = sb("negmax", [P, ET])
        zsum = sb("zsum", [P, ET])
        zinv = sb("zinv", [P, ET])
        rw = sb("rw", [P, ET, QS])
        ew = sb("ew", [P, 2, S])
        pt = sb("pt", [P, 2, NT, P])
        g_sb = sb("g_sb", [P, NT, NT, P])
        sel_sb = sb("sel_sb", [P, QS])
        id_sb = sb("id_sb", [P, P])
        z2inv = sb("z2inv", [P, NT])
        turn = sb("turn", [P, 1])
        one = sb("one", [P, 1])
        res = sb("res", [P, NT, E])
        bn = sb("bn", [P, 4, NT, 6])
        mv = sb("mv", [P, 4, NT, 2])
        veps = sb("veps", [P, 4, NT])
        rstd = sb("rstd", [P, 4, NT])
        nhalf = sb("nhalf", [P, NT])
        xh1 = sb("xh1", [P, NT, E])
        aff = sb("aff", [P, NT, E])
        xh2 = sb("xh2", [P, NT, E])
        h2t = sb("h2t", [P, S])
        h2r = sb("h2r", [P, S])
        relu = sb("relu", [P, CH, S])
        xh3 = sb("xh3", [P, NT, E])
        h3 = sb("h3", [P, NT, E])
        qf = sb("qf", [P, S])
        kf = sb("kf", [P, S])
        qhi, qlo = sb("qhi", [P, S], f32r), sb("qlo", [P, S], f32r)
        khi, klo = sb("khi", [P, S], f32r), sb("klo", [P, S], f32r)
        xin = [sb(f"xin{i}", [P, NT, E]) for i in range(2)]
        wqk_sb = sb("wqk_sb", [P, 2, E])
        bqk_sb = sb("bqk_sb", [P, 2])
        w1_sb = sb("w1_sb", [P, F])
        w2_sb = sb("w2_sb", [P, CH, E])
        col = sb("col", [P, NCOL])
        row = sb("row", [P, 4, E])
        att = ctx.enter_context(ExitStack())

        def att_sb(name, shape, dt=f32):
            return att.enter_context(nc.sbuf_tensor(name, shape, dt))

        qb = [att_sb(f"qb{i}", [96, NG, HG, S], f32r) for i in range(2)]
        kb = [att_sb(f"kb{i}", [96, NG, S], f32r) for i in range(2)]
        att.close()
        gate = [sb(f"gate{i}", [P, CH, S]) for i in range(2)]
        hid = [sb(f"hid{i}", [P, CH, S]) for i in range(2)]
        hid2 = [sb(f"hid_b{i}", [P, CH, S]) for i in range(2)]
        fh1_sb, fh2_sb = sb("fh1_sb", [P, CH, F]), sb("fh2_sb", [P, CH, F])
        fw1_sb, fw2_sb = sb("fw1_sb", [P, F]), sb("fw2_sb", [P, F])
        fw3_sb = sb("fw3_sb", [P, CH, E])
        fcol = sb("fcol", [P, 4, CH])
        frow_sb = sb("frow_sb", [P, E])
        y_sb = [sb(f"y{i}", [P, NT, E]) for i in range(2)]

        sc = [ctx.enter_context(nc.psum_tensor(f"sc{i}", [P, S], f32)) for i in range(NS)]
        mean = ctx.enter_context(nc.psum_tensor("mean", [P, S], f32))
        m0 = ctx.enter_context(nc.psum_tensor("m0", [P, S], f32))
        m1 = ctx.enter_context(nc.psum_tensor("m1", [P, S], f32))
        sa_bank = [m1, m0, m1, m1]
        banks = [*sc, mean, m0, m1]

        const_loaded = sem("const_loaded")
        qkw_loaded = sem("qkw_loaded")
        filled = sem("filled")
        x_loaded = [sem(f"x_loaded{i}") for i in range(2)]
        layer_loaded = sem("layer_loaded")
        net_loaded = sem("net_loaded")
        qk_loaded = [sem(f"qk_loaded{i}") for i in range(2)]
        hc_loaded = [sem(f"hc_loaded{i}") for i in range(2)]
        kept = sem("kept")
        scores_ready = sem("scores_ready")
        max_ready = sem("max_ready")
        exp_ready = sem("exp_ready")
        zinv_ready = sem("zinv_ready")
        weights_ready = sem("weights_ready")
        summed = sem("summed")
        ew_ready = sem("ew_ready")
        ewt_ready = sem("ewt_ready")
        pt_ready = sem("pt_ready")
        sa_ready = sem("sa_ready")
        z2_ready = sem("z2_ready")
        res_ready = sem("res_ready")
        bn_ready = [sem(f"bn_ready{i}") for i in range(4)]
        mv_ready = [sem(f"mv_ready{i}") for i in range(4)]
        veps_ready = [sem(f"veps_ready{i}") for i in range(4)]
        rstd_ready = [sem(f"rstd_ready{i}") for i in range(4)]
        xh_ready = [sem(f"xh_ready{i}") for i in range(4)]
        h1a_ready, h1_ready = sem("h1a_ready"), sem("h1_ready")
        xh2t_ready = sem("xh2t_ready")
        h2t_ready, h2r_ready = sem("h2t_ready"), sem("h2r_ready")
        up_ready, relu_ready = sem("up_ready"), sem("relu_ready")
        down_ready = sem("down_ready")
        h3a_ready, h3_ready = sem("h3a_ready"), sem("h3_ready")
        xh3t_ready, ht_ready = sem("xh3t_ready"), sem("ht_ready")
        q_ready, k_ready = sem("q_ready"), sem("k_ready")
        qf_ready, kf_ready = sem("qf_ready"), sem("kf_ready")
        qhi_ready, khi_ready = sem("qhi_ready"), sem("khi_ready")
        split_ready = sem("split_ready")
        y_ready = sem("y_ready")
        g_mm, g_silu, g_hid = sem("g_mm"), sem("g_silu"), sem("g_hid")
        g_a, g_b = sem("g_a"), sem("g_b")
        g_gelu = sem("g_gelu")
        g_out, g_scaled, g_done = sem("g_out"), sem("g_scaled"), sem("g_done")
        y_loaded = [sem(f"y_loaded{i}") for i in range(2)]
        stored = sem("stored")

        def bank_user(j):
            if j >= NS:
                return j - NS
            last = [n for n in range(TILES) if n % NS == j][-1]
            return last - TILES

        def permuted(q):
            return q[:, :].rearrange("p (k i n) -> p i n k", i=NT, n=4)

        def by_tile(q):
            return q[:, :].rearrange("p (i n k) -> p i n k", i=NT, n=4)

        def wait_later(engine, what, count):
            if type(count) is not int or count > 0:
                engine.wait_ge(what, count)

        block = ctx.enter_context(nc.Block())

        @block.sync
        def _(sp):
            sp.dma_start(wqk_sb[:, :, :], wqk[0]).then_inc(qkw_loaded, 16)
            sp.dma_start(bqk_sb[:, :], bqk[0]).then_inc(qkw_loaded, 16)
            sp.dma_start(id_sb[:, :], ident).then_inc(const_loaded, 16)
            sp.dma_start(g_sb[:, :, :, :], gmat).then_inc(const_loaded, 16)
            sp.dma_start(sel_sb[:, :], sel).then_inc(const_loaded, 16)

            def load_x(b, n, par):
                sp.dma_start(xin[par][:, :, :], x[bass.ds(b, 1), :, :, :].rearrange("a p t e -> p (a t) e")) \
                    .then_inc(x_loaded[par], 16)

            def store_split(b):
                for n, part in enumerate((qhi, qlo, khi, klo)):
                    sp.dma_start(qk_dram[bass.ds(b, 1), n, :, :].rearrange("a p s -> (a p) s"),
                                 part[:, :].bitcast(f32)).then_inc(kept, 16)

            def load_split(b, par):
                for part, src in enumerate((2, 3, 2)):
                    sp.dma_start(kb[par][32 * part:32 * part + 32, :, :].bitcast(f32),
                                 qk_dram[bass.ds(b, 1), src, :, :].rearrange("a (g r) s -> r (a g) s", g=NG)) \
                        .then_inc(qk_loaded[par], 16)
                for part, src in enumerate((0, 0, 1)):
                    for h in range(HG):
                        r = 32 * part + DH * h
                        sp.dma_start(qb[par][r:r + DH, :, h, :].bitcast(f32),
                                     qk_dram[bass.ds(b, 1), src, :, :]
                                     .rearrange("a (g h r) s -> h r (a g) s", g=NG, h=HG)[h]) \
                            .then_inc(qk_loaded[par], 16)

            def load_tokens(b, par):
                sp.dma_start(hc[par][:, :, 0:E], hs[:, bass.ds(b, 1), :, :].rearrange("p a t e -> p (a t) e")) \
                    .then_inc(hc_loaded[par], 16)

            for b in range(2):
                load_x(b, 0, b)
            def first_pair(v):
                for par in range(2):
                    b = v * 2 + par
                    sp.wait_ge(xh_ready[3], b + 1)
                    load_x((b + 2) % B, 0, par)
                    sp.wait_ge(split_ready, b * 2 + 2)
                    store_split(b)

            first_pair(0)
            with sp.Fori(1, B // 2) as v:
                first_pair(v)
            sp.wait_ge(kept, 64 * B)
            sp.wait_ge(filled, 4)
            sp.wait_ge(h3_ready, B)
            for t in range(2):
                load_split(t, t)
                load_tokens(t, t)

            def load_layer(n, project):
                sp.wait_ge(kf_ready, n * B + B)
                sp.wait_ge(qf_ready, n * B + B)
                sp.wait_ge(h3_ready, n * B + B)
                one = bass.ds(n, 1)
                sp.dma_start(w1_sb[:, :], w1t[one, :, :].rearrange("a p f -> p (a f)")).then_inc(layer_loaded, 16)
                sp.dma_start(w2_sb[:, :, :], w2t[one, :, :, :].rearrange("a p c e -> p (a c) e")).then_inc(layer_loaded, 16)
                sp.dma_start(col[:, :], cols[one, :, :].rearrange("a p c -> p (a c)")).then_inc(layer_loaded, 16)
                sp.dma_start(row[:, :, :], rows[one, :, :].to_broadcast([P, 4, E])).then_inc(layer_loaded, 16)
                if project:
                    nxt = bass.ds(n + 1, 1)
                    sp.dma_start(wqk_sb[:, :, :], wqk[nxt, :, :, :].rearrange("a p c e -> p (a c) e")).then_inc(layer_loaded, 16)
                    sp.dma_start(bqk_sb[:, :], bqk[nxt, :, :].rearrange("a p c -> p (a c)")).then_inc(layer_loaded, 16)

            def body(u, par, project, load):
                if load:
                    sp.wait_ge(scores_ready, u * TILES + TILES)
                    load_split((u + 2) % B, par)
                    sp.wait_ge(res_ready, u * NT + NT)
                    load_tokens((u + 2) % B, par)
                if project:
                    sp.wait_ge(split_ready, u * 2 + 2 * B + 2)
                    store_split(u % B)
                else:
                    sp.wait_ge(y_ready, u - (U - B) + 1)
                    sp.dma_start(y_dram[bass.ds(u % B, 1), :, :, :].rearrange("a p t e -> p (a t) e"), h3[:, :, :]) \
                        .then_inc(kept, 16)

            with sp.Fori(0, D - 1) as n:
                load_layer(n, True)
                with sp.Fori(0, B // 2) as v:
                    for par in range(2):
                        body(n * B + v * 2 + par, par, True, True)
            load_layer(D - 1, False)
            sp.wait_ge(kept, U * 64)

            def load_x_again(u, par):
                sp.dma_start(xin[par][:, :, :], x[bass.ds(u % B, 1), :, :, :].rearrange("a p t e -> p (a t) e")) \
                    .then_inc(x_loaded[par], 16)

            with sp.Fori(0, B // 2 - 1) as v:
                for par in range(2):
                    u = v * 2 + (U - B) + par
                    body(u, par, False, True)
                    load_x_again(u + 2, par)
            body(U - 2, 0, False, False)
            sp.wait_ge(scores_ready, U * TILES)
            for dst, src in ((fw1_sb[:, :], fw1), (fw2_sb[:, :], fw2), (fh1_sb[:, :, :], fh1), (fh2_sb[:, :, :], fh2),
                             (fw3_sb[:, :, :], fw3), (fcol[:, :, :], fcols), (frow_sb[:, :], frow.to_broadcast([P, E]))):
                sp.dma_start(dst, src).then_inc(net_loaded, 16)
            body(U - 1, 1, False, False)

            def load_y(b, par):
                sp.dma_start(y_sb[par][:, :, :], y_dram[bass.ds(b, 1), :, :, :].rearrange("a p t e -> p (a t) e")) \
                    .then_inc(y_loaded[par], 16)

            sp.wait_ge(kept, 64 * U + 16 * B)
            load_y(0, 0)
            load_y(1, 1)
            def net_pair(v):
                for par in range(2):
                    b = v * 2 + par
                    sp.wait_ge(g_done, b + 1)
                    sp.dma_start(out[bass.ds(b, 1), :, :, :].rearrange("a p t e -> p (a t) e"), y_sb[par][:, :, :]) \
                        .then_inc(stored, 16)
                    sp.wait_ge(stored, b * 16 + 16)
                    load_y((b + 2) % B, par)

            net_pair(0)
            with sp.Fori(1, B // 2) as v:
                net_pair(v)
            for par in range(2):
                sp.wait_ge(y_loaded[par], 16 * (B // 2 + 1))

        @block.gpsimd
        def _(gp):
            gp.memset(one[:, :], 1.0)
            gp.memset(nhalf[:, :], -0.5).then_inc(filled, 1)
            for i in range(2):
                gp.memset(hc[i][:, :, E:E + 1], 1.0)
                gp.memset(qb[i][:, :, :, :].bitcast(f32), 0.0).then_inc(filled, 1)
            gp.memset(negmax[:, :], 0.0).then_inc(filled, 1)
            gp.wait_ge(filled, 4)

            def power(k, n):
                gp.wait_ge(veps_ready[k], n)
                nc.gpsimd.tensor_tensor(rstd[:, k, :], veps[:, k, :], nhalf[:, :], ALU.pow).then_inc(rstd_ready[k], 1)

            def low_part(full, high, low, full_ready, high_ready, n):
                gp.wait_ge(full_ready, n)
                nc.gpsimd.tensor_tensor(high[:, :], full[:, :], one[:, 0:1].to_broadcast([P, S]), ALU.mult) \
                    .then_inc(high_ready, 1)
                gp.wait_ge(high_ready, n)
                nc.gpsimd.tensor_tensor(low[:, :], full[:, :], high[:, :].bitcast(f32), ALU.subtract) \
                    .then_inc(split_ready, 1)

            def first_pair(v):
                for par in range(2):
                    b = v * 2 + par
                    power(3, b + 1)
                    gp.wait_ge(xh_ready[3], b + 1)
                    nc.gpsimd.tensor_copy(hs[:, bass.ds(b, 1), :, :].rearrange("p a t e -> p (a t e)"),
                                          xh3[:, :, :].rearrange("p t e -> p (t e)")).then_inc(h3_ready, 1)

            first_pair(0)
            with gp.Fori(1, B // 2) as v:
                first_pair(v)

            def body(u, project):
                gp.wait_ge(layer_loaded, (u // B) * 96 + (96 if project else 64))
                power(0, u + 1)
                gp.wait_ge(xh_ready[0], u + 1)
                nc.gpsimd.tensor_tensor(aff[:, :, :], xh1[:, :, :], row[:, 0:1, :].to_broadcast([P, NT, E]), ALU.mult) \
                    .then_inc(h1a_ready, 1)
                gp.wait_ge(h1a_ready, u + 1)
                nc.gpsimd.tensor_tensor(aff[:, :, :], aff[:, :, :], row[:, 1:2, :].to_broadcast([P, NT, E]), ALU.add) \
                    .then_inc(h1_ready, 1)
                power(1, u + 1)
                gp.wait_ge(h2t_ready, u + 1)
                nc.gpsimd.tensor_tensor(h2r[:, :], h2t[:, :], col[:, C_B2:C_B2 + 1].to_broadcast([P, S]), ALU.add) \
                    .then_inc(h2r_ready, 1)
                power(2, u + 1)
                gp.wait_ge(xh_ready[2], u + 1)
                nc.gpsimd.tensor_tensor(aff[:, :, :], xh3[:, :, :], row[:, 2:3, :].to_broadcast([P, NT, E]), ALU.mult) \
                    .then_inc(h3a_ready, 1)
                gp.wait_ge(h3a_ready, u + 1)
                if project:
                    nc.gpsimd.tensor_tensor(hs[:, bass.ds(u % B, 1), :, :].rearrange("p a t e -> p (a t) e"),
                                            aff[:, :, :], row[:, 3:4, :].to_broadcast([P, NT, E]), ALU.add) \
                        .then_inc(h3_ready, 1)
                    gp.wait_ge(kept, u * 64 + 64 * B)
                    low_part(qf, qhi, qlo, qf_ready, qhi_ready, u + B + 1)
                    low_part(kf, khi, klo, kf_ready, khi_ready, u + B + 1)

            def last_body(u, par):
                body(u, False)
                n = u - (U - B)
                nc.gpsimd.tensor_tensor(aff[:, :, :], aff[:, :, :], row[:, 3:4, :].to_broadcast([P, NT, E]), ALU.add) \
                    .then_inc(h3_ready, 1)
                gp.wait_ge(h3_ready, u + B + 1)
                gp.wait_ge(x_loaded[par], (n // 2) * 16 + (B // 2 + 1) * 16)
                gp.wait_ge(kept, n * 16 + 64 * U)
                nc.gpsimd.tensor_tensor(h3[:, :, :], aff[:, :, :], xin[par][:, :, :], ALU.add).then_inc(y_ready, 1)
                power(3, u - (U - B) + B + 1)

            with gp.Fori(0, (U - B) // 2) as v:
                for par in range(2):
                    body(v * 2 + par, True)
            with gp.Fori(0, B // 2 - 1) as v:
                for par in range(2):
                    last_body(v * 2 + (U - B) + par, par)
            last_body(U - 2, 0)
            last_body(U - 1, 1)

        @block.vector
        def _(dve):
            def split(full, high, low, full_ready, high_ready, n):
                dve.wait_ge(full_ready, n)
                nc.vector.tensor_copy(high[:, :], full[:, :]).then_inc(high_ready, 1)
                dve.wait_ge(high_ready, n)
                nc.vector.tensor_tensor(low[:, :], full[:, :], high[:, :].bitcast(f32), ALU.subtract) \
                    .then_inc(split_ready, 1)

            def stats(src, k, i, src_ready, n, last):
                dve.wait_ge(src_ready, n)
                ins = nc.vector.bn_stats(bn[:, k, i, :], src)
                if last:
                    ins.then_inc(bn_ready[k], 1)

            def spread(k, n):
                for i in range(NT):
                    ins = nc.vector.bn_aggr(mv[:, k, i, :], bn[:, k, i, :])
                ins.then_inc(mv_ready[k], 1)
                dve.wait_ge(mv_ready[k], n)
                nc.vector.tensor_scalar(veps[:, k, :], mv[:, k, :, 1], EPS, None, ALU.add).then_inc(veps_ready[k], 1)

            def apply(dst, src, k, n):
                dve.wait_ge(rstd_ready[k], n)
                for i in range(NT):
                    ins = nc.vector.tensor_scalar(dst[:, i, :], src(i), mv[:, k, i, 0:1], rstd[:, k, i:i + 1],
                                                  ALU.subtract, ALU.mult)
                ins.then_inc(xh_ready[k], 1)

            dve.wait_ge(qkw_loaded, 32)
            dve.wait_ge(filled, 4)
            def first_pair(v):
                for par in range(2):
                    b = v * 2 + par
                    for i in range(NT):
                        stats(xin[par][:, i, :], 3, i, x_loaded[par], v * 16 + 16, i == NT - 1)
                    dve.wait_ge(bn_ready[3], b + 1)
                    nc.vector.memset(turn[:, :], 0.0)
                    spread(3, b + 1)
                    wait_later(dve, h3_ready, b)
                    wait_later(dve, xh3t_ready, b)
                    apply(xh3, lambda i: xin[par][:, i, :], 3, b + 1)
                    dve.wait_ge(q_ready, b + 1)
                    nc.vector.tensor_scalar(permuted(qf), by_tile(m0), bqk_sb[:, 0:1], DH ** -0.5, ALU.add, ALU.mult) \
                        .then_inc(qf_ready, 1)
                    wait_later(dve, kept, b * 64)
                    split(qf, qhi, qlo, qf_ready, qhi_ready, b + 1)
                    split(kf, khi, klo, kf_ready, khi_ready, b + 1)

            first_pair(0)
            with dve.Fori(1, B // 2) as v:
                first_pair(v)

            def score_max(t, j):
                dve.wait_ge(scores_ready, t * TILES + j + 1)
                nc.vector.tensor_reduce(negmax[:, j % ET:j % ET + 1], sc[j % NS][:, :], AX, ALU.max, negate=True) \
                    .then_inc(max_ready, 1)

            def invert_sums(t, q):
                dve.wait_ge(exp_ready, t * TILES + 4 * q + 4)
                c = 4 * q % ET
                nc.vector.reciprocal(zinv[:, c:c + 4], zsum[:, c:c + 4]).then_inc(zinv_ready, 1)

            def row_weights(t, q):
                dve.wait_ge(zinv_ready, t * NQ + q + 1)
                c = 4 * q % ET
                nc.vector.tensor_tensor(rw[:, c:c + 4, :],
                                        sel_sb[:, :].rearrange("p (a q) -> p a q", a=1).to_broadcast([P, 4, QS]),
                                        zinv[:, c:c + 4].rearrange("p (a q) -> p a q", q=1).to_broadcast([P, 4, QS]),
                                        ALU.mult).then_inc(weights_ready, 1)

            def relative(t, i):
                dve.wait_ge(ewt_ready, t * NT + i + 1)
                nc.vector.tensor_tensor(pt[:, i % 2, :, :], m0[:, :].rearrange("p (c l) -> p c l", c=NT),
                                        g_sb[:, i, :, :], ALU.mult).then_inc(pt_ready, 1)

            def invert_row(t, i):
                dve.wait_ge(sa_ready, t * NT + i + 1)
                nc.vector.reciprocal(z2inv[:, i:i + 1], sa_bank[i][:, E:E + 1]).then_inc(z2_ready, 1)

            def residual(t, i, par):
                dve.wait_ge(z2_ready, t * NT + i + 1)
                nc.vector.scalar_tensor_tensor(res[:, i, :], sa_bank[i][:, 0:E], z2inv[:, i:i + 1],
                                               hc[par][:, i, 0:E], ALU.mult, ALU.add).then_inc(res_ready, 1)

            def body(u, par, tail, scores, project):
                t, tp = u + 1, 1 - par
                if tail:
                    dve.wait_ge(layer_loaded, (u // B) * 96 + (96 if project else 64))
                for j in range(TILES):
                    for k, at in ((0, 19), (1, 28), (2, 49), (3, 58)):
                        if tail and j == at and k < 3:
                            dve.wait_ge(bn_ready[k], u + 1)
                        if tail and j == at and k == 3 and not project:
                            dve.wait_ge(bn_ready[3], u - (U - B) + B + 1)
                    if scores:
                        score_max(t, j)
                    if j == 1 and tail:
                        invert_sums(u, NQ - 1)
                    if j == 2 and tail:
                        row_weights(u, NQ - 1)
                    if j % 4 == 1 and j > 4 and scores:
                        invert_sums(t, j // 4 - 1)
                    if j % 4 == 2 and j > 4 and scores:
                        row_weights(t, j // 4 - 1)
                    for i, at, n, on, pn in ((2, 0, u, tail, par), (3, 16, u, tail, par),
                                             (0, 32, t, scores, tp), (1, 52, t, scores, tp)):
                        if on and j == at:
                            invert_row(n, i)
                        if on and j == at + 1:
                            residual(n, i, pn)
                        if on and j == at + 2:
                            stats(res[:, i, :], 0, i, res_ready, n * NT + i + 1, i == NT - 1)
                    for i, at, n, on in ((3, 12, u, tail), (0, 28, t, scores), (1, 44, t, scores), (2, 60, t, scores)):
                        if on and j == at:
                            relative(n, i)
                    if not tail:
                        continue
                    if j == 19:
                        spread(0, u + 1)
                    if j == 22:
                        apply(xh1, lambda i: res[:, i, :], 0, u + 1)
                    if j == 27:
                        for i in range(NT):
                            stats(aff[:, i, :], 1, i, h1_ready, u + 1, i == NT - 1)
                    if j == 28:
                        spread(1, u + 1)
                    if j == 31:
                        apply(xh2, lambda i: aff[:, i, :], 1, u + 1)
                    if j == 35:
                        dve.wait_ge(xh2t_ready, u + 1)
                        nc.vector.tensor_scalar(h2t[:, :], m0[:, :], col[:, C_W2:C_W2 + 1], col[:, C_BB2:C_BB2 + 1],
                                                ALU.mult, ALU.add).then_inc(h2t_ready, 1)
                    if j == 48:
                        for i in range(NT):
                            stats(m1[:, i * E:i * E + E], 2, i, down_ready, u + 1, i == NT - 1)
                    if j == 49:
                        spread(2, u + 1)
                    if j == 51:
                        apply(xh3, lambda i: m1[:, i * E:i * E + E], 2, u + 1)
                    if project and j == 58:
                        dve.wait_ge(xh3t_ready, u + B + 1)
                        nc.vector.tensor_scalar(h2t[:, :], m0[:, :], col[:, C_W3:C_W3 + 1], col[:, C_BB3:C_BB3 + 1],
                                                ALU.mult, ALU.add).then_inc(ht_ready, 1)
                    if project and j == 62:
                        dve.wait_ge(q_ready, u + B + 1)
                        nc.vector.tensor_scalar(permuted(qf), by_tile(m1), bqk_sb[:, 0:1], DH ** -0.5, ALU.add, ALU.mult) \
                            .then_inc(qf_ready, 1)
                    if not project and j == 57:
                        n = u - (U - B) + B + 1
                        for i in range(NT):
                            stats(h3[:, i, :], 3, i, y_ready, n - B, i == NT - 1)
                    if not project and j == 58:
                        spread(3, u - (U - B) + B + 1)
                    if not project and j == 61:
                        apply(xh3, lambda i: h3[:, i, :], 3, u - (U - B) + B + 1)

            body(-1, 1, False, True, True)
            with dve.Fori(0, (U - B) // 2) as v:
                for par in range(2):
                    body(v * 2 + par, par, True, True, True)
            with dve.Fori((U - B) // 2, U // 2 - 1) as v:
                for par in range(2):
                    body(v * 2 + par, par, True, True, False)
            body(U - 2, 0, True, True, False)
            body(U - 1, 1, True, False, False)

            dve.wait_ge(net_loaded, 7 * 16)
            def net_pair(v):
                for par in range(2):
                    b = v * 2 + par
                    for c in range(CH):
                        dve.wait_ge(g_silu, b * CH + c + 1)
                        nc.vector.scalar_tensor_tensor(hid[par][:, c, :], banks[4 + c % 2][:, :], fcol[:, 1, c:c + 1],
                                                       gate[par][:, c, :], ALU.mult, ALU.mult).then_inc(g_hid, 1)
                for par in range(2):
                    b = v * 2 + par
                    dve.wait_ge(g_out, b + 1)
                    nc.vector.tensor_tensor(gate[par][:, :, 0:E], banks[6 + par][:, :].rearrange("p (t e) -> p t e", t=NT),
                                            frow_sb[:, :].rearrange("p (a e) -> p a e", a=1).to_broadcast([P, NT, E]),
                                            ALU.mult).then_inc(g_scaled, 1)
                    dve.wait_ge(g_scaled, b + 1)
                    dve.wait_ge(y_loaded[par], v * 16 + 16)
                    nc.vector.tensor_tensor(y_sb[par][:, :, :], y_sb[par][:, :, :], gate[par][:, :, 0:E], ALU.add) \
                        .then_inc(g_done, 1)

            net_pair(0)
            with dve.Fori(1, B // 2) as v:
                net_pair(v)

        @block.scalar
        def _(act):
            act.wait_ge(qkw_loaded, 32)
            def first_pair(v):
                for par in range(2):
                    b = v * 2 + par
                    act.wait_ge(xh3t_ready, b + 1)
                    nc.scalar.activation(h2t[:, :], m1[:, :], ACT.Copy).then_inc(ht_ready, 1)
                    act.wait_ge(k_ready, b + 1)
                    wait_later(act, split_ready, b * 2)
                    nc.scalar.activation(kf[:, :], mean[:, :], ACT.Identity, bias=bqk_sb[:, 1:2]).then_inc(kf_ready, 1)

            first_pair(0)
            with act.Fori(1, B // 2) as v:
                first_pair(v)

            def exp_scores(t, j):
                act.wait_ge(max_ready, t * TILES + j + 1)
                if j % 4 == 0 and (type(t) is not int or t > 0 or j >= ET):
                    act.wait_ge(summed, t * NQ + j // 4 - 3)
                c = j % ET
                nc.scalar.activation(ex[:, c, :], sc[j % NS][:, :], ACT.Exp, bias=negmax[:, c:c + 1],
                                     accum_out=zsum[:, c:c + 1]).then_inc(exp_ready, 1)

            def exp_mean(t, i):
                act.wait_ge(summed, t * NQ + 4 * i + 4)
                if type(t) is not int or t > 0 or i >= 2:
                    act.wait_ge(ewt_ready, t * NT + i - 1)
                nc.scalar.activation(ew[:, i % 2, :], mean[:, :], ACT.Exp).then_inc(ew_ready, 1)

            def body(u, par, tail, scores, project):
                t = u + 1
                if tail:
                    act.wait_ge(layer_loaded, (u // B) * 96 + (96 if project else 64))
                for j in range(TILES):
                    if scores:
                        exp_scores(t, j)
                    if j == 6 and tail:
                        exp_mean(u, 3)
                    if j in (22, 38, 54) and scores:
                        exp_mean(t, j // 16 - 1)
                    for c, at in ((0, 36), (1, 37), (2, 40), (3, 41)):
                        if tail and j == at:
                            act.wait_ge(up_ready, u * CH + c + 1)
                            nc.scalar.activation(relu[:, c, :], (m1 if c % 2 == 0 else m0)[:, :], ACT.Relu,
                                                 bias=col[:, C_B1 + c:C_B1 + c + 1]).then_inc(relu_ready, 1)
                if tail and project:
                    act.wait_ge(k_ready, u + B + 1)
                    act.wait_ge(split_ready, u * 2 + 2 * B)
                    nc.scalar.activation(kf[:, :], m0[:, :], ACT.Identity, bias=bqk_sb[:, 1:2]).then_inc(kf_ready, 1)
                if tail and not project:
                    act.wait_ge(xh3t_ready, u - (U - B) + U + 1)
                    nc.scalar.activation(hs[:, bass.ds(u % B, 1), :, :].rearrange("p a t e -> p (a t e)"), m0[:, :],
                                         ACT.Copy).then_inc(ht_ready, 1)

            body(-1, 1, False, True, True)
            with act.Fori(0, (U - B) // 2) as v:
                for par in range(2):
                    body(v * 2 + par, par, True, True, True)
            with act.Fori((U - B) // 2, U // 2 - 1) as v:
                for par in range(2):
                    body(v * 2 + par, par, True, True, False)
            body(U - 2, 0, True, True, False)
            body(U - 1, 1, True, False, False)

            act.wait_ge(net_loaded, 7 * 16)
            def net_pair(v):
                for par in range(2):
                    b = v * 2 + par
                    for c in range(CH):
                        act.wait_ge(g_mm, b * 2 * CH + 2 * c + 2)
                        wait_later(act, g_done, v * 2)
                        nc.scalar.activation(gate[par][:, c, :], banks[2 + c % 2][:, :], ACT.Silu,
                                             scale=fcol[:, 0, c:c + 1]).then_inc(g_silu, 1)
                for k, product, dst in ((2, g_a, hid2), (3, g_b, hid)):
                    for par in range(2):
                        b = v * 2 + par
                        for c in range(CH):
                            act.wait_ge(product, b * CH + c + 1)
                            nc.scalar.activation(dst[par][:, c, :], banks[c % 2][:, :], ACT.Gelu,
                                                 scale=fcol[:, k, c:c + 1]).then_inc(g_gelu, 1)

            net_pair(0)
            with act.Fori(1, B // 2) as v:
                net_pair(v)

        @block.tensor
        def _(pe):
            pe.wait_ge(const_loaded, 48)
            pe.wait_ge(qkw_loaded, 32)
            def first_pair(v):
                for par in range(2):
                    b = v * 2 + par
                    pe.wait_ge(xh_ready[3], b + 1)
                    for i in range(NT):
                        ins = nc.tensor.transpose(m1[:, i * P:i * P + P], xh3[:, i, :], id_sb[:, :])
                    ins.then_inc(xh3t_ready, 1)
                    pe.wait_ge(ht_ready, b + 1)
                    wait_later(pe, qf_ready, b)
                    nc.tensor.matmul(m0[:, :], wqk_sb[:, 0, :], h2t[:, :], start=True, stop=True).then_inc(q_ready, 1)
                    wait_later(pe, kf_ready, b)
                    nc.tensor.matmul(mean[:, :], wqk_sb[:, 1, :], h2t[:, :], start=True, stop=True).then_inc(k_ready, 1)

            first_pair(0)
            with pe.Fori(1, B // 2) as v:
                first_pair(v)

            def score_tile(t, j, par):
                q, n = j // 4, j % 4
                i, g = q // NG, q % NG
                free = bank_user(j)
                if type(t) is not int or t > 0 or free >= 0:
                    pe.wait_ge(exp_ready, t * TILES + free + 1)
                flat = qb[par][:, g, :, :].rearrange("r h s -> r (h s)")
                nc.tensor.matmul(sc[j % NS][:, :], flat[:, NT * i + n::S // QS], kb[par][:, g, :], start=True, stop=True) \
                    .then_inc(scores_ready, 1)

            def sum_heads(t, q):
                pe.wait_ge(weights_ready, t * NQ + q + 1)
                i, g = q // NG, q % NG
                if g == 0 and (type(t) is not int or t > 0 or i > 0):
                    pe.wait_ge(ew_ready, t * NT + i)
                for n in range(4):
                    c = (4 * q + n) % ET
                    ins = nc.tensor.matmul(mean[n * QS:(n + 1) * QS, :], rw[:, c, :], ex[:, c, :],
                                           start=(g == 0), stop=(g == NG - 1))
                ins.then_inc(summed, 1)

            def transpose_mean(t, i):
                pe.wait_ge(ew_ready, t * NT + i + 1)
                for c in range(NT):
                    ins = nc.tensor.transpose(m0[:, c * P:c * P + P], ew[:, i % 2, c * P:c * P + P], id_sb[:, :])
                ins.then_inc(ewt_ready, 1)

            def attend(t, i, par, loaded):
                pe.wait_ge(hc_loaded[par], loaded)
                pe.wait_ge(pt_ready, t * NT + i + 1)
                for c in range(NT):
                    ins = nc.tensor.matmul(sa_bank[i][:, 0:E + 1], pt[:, i % 2, c, :], hc[par][:, c, :],
                                           start=(c == 0), stop=(c == NT - 1))
                ins.then_inc(sa_ready, 1)

            def up(u, c):
                nc.tensor.matmul((m1 if c % 2 == 0 else m0)[:, :], w1_sb[:, c * P:c * P + P], h2t[:, :],
                                 start=True, stop=True).then_inc(up_ready, 1)

            def down(i):
                dst = m1[:, i * E:i * E + E]
                nc.tensor.matmul(dst, h2r[:, i * P:i * P + P], id_sb[:, :], start=True, stop=False)
                for c in range(CH):
                    ins = nc.tensor.matmul(dst, relu[:, c, i * P:i * P + P], w2_sb[:, c, :], start=False, stop=(c == CH - 1))
                return ins

            def body(u, par, pair, tail, scores, project):
                t, tp = u + 1, 1 - par
                tpair = pair + par if tail else 0
                if tail:
                    pe.wait_ge(layer_loaded, (u // B) * 96 + (96 if project else 64))
                for s in range(NQ):
                    if scores:
                        if s == 0:
                            pe.wait_ge(qk_loaded[tp], tpair * (16 * LOADS) + 16 * LOADS)
                        for n in range(4):
                            score_tile(t, 4 * s + n, tp)
                    if s < 2 and tail:
                        sum_heads(u, NQ - 2 + s)
                    if s >= 2 and scores:
                        sum_heads(t, s - 2)
                    if s == 2 and tail:
                        transpose_mean(u, 3)
                    if s == 3 and tail:
                        pe.wait_ge(res_ready, u * NT + 3)
                        attend(u, 3, par, pair * 16 + 16)
                    if s in (6, 10, 14) and scores:
                        i = s // 4 - 1
                        if tail and i == 1:
                            pe.wait_ge(relu_ready, u * CH + 4)
                        if tail and i == 2 and project:
                            pe.wait_ge(ht_ready, u + B + 1)
                        if i == 2 and not (tail and project):
                            pe.wait_ge(res_ready, t * NT + 2)
                        transpose_mean(t, i)
                    if s in (7, 12) and scores:
                        i = 0 if s == 7 else 1
                        if i == 0 and tail:
                            pe.wait_ge(res_ready, t * NT)
                        attend(t, i, tp, tpair * 16 + 16)
                    if s == 7 and tail:
                        pe.wait_ge(xh_ready[1], u + 1)
                        for i in range(NT):
                            ins = nc.tensor.transpose(m0[:, i * P:i * P + P], xh2[:, i, :], id_sb[:, :])
                        ins.then_inc(xh2t_ready, 1)
                    if s == 8 and tail:
                        pe.wait_ge(h2t_ready, u + 1)
                        if scores:
                            pe.wait_ge(res_ready, t * NT + 1)
                        up(u, 0)
                        up(u, 1)
                    if s == 9 and tail:
                        pe.wait_ge(relu_ready, u * CH + 1)
                        up(u, 2)
                        pe.wait_ge(relu_ready, u * CH + 2)
                        up(u, 3)
                    if s == 10 and tail:
                        pe.wait_ge(relu_ready, u * CH + 4)
                        pe.wait_ge(h2r_ready, u + 1)
                        down(0)
                        down(1)
                    if s == 11 and tail:
                        down(2)
                        down(3).then_inc(down_ready, 1)
                    if s == 13 and tail and project:
                        pe.wait_ge(xh_ready[2], u + 1)
                        if scores:
                            pe.wait_ge(res_ready, t * NT + 2)
                        for i in range(NT):
                            ins = nc.tensor.transpose(m0[:, i * P:i * P + P], xh3[:, i, :], id_sb[:, :])
                        ins.then_inc(xh3t_ready, 1)
                    if s == 14 and tail and project:
                        nc.tensor.matmul(m1[:, :], wqk_sb[:, 0, :], h2t[:, :], start=True, stop=True).then_inc(q_ready, 1)
                    if s == 15 and scores:
                        if tail and project:
                            pe.wait_ge(qf_ready, u + B + 1)
                        elif tail:
                            pe.wait_ge(xh_ready[2], u + 1)
                        attend(t, 2, tp, tpair * 16 + 16)
                    if s == 15 and tail and project:
                        nc.tensor.matmul(m0[:, :], wqk_sb[:, 1, :], h2t[:, :], start=True, stop=True).then_inc(k_ready, 1)
                    if s == 15 and tail and not project:
                        pe.wait_ge(xh_ready[3], u - (U - B) + B + 1)
                        for i in range(NT):
                            ins = nc.tensor.transpose(m0[:, i * P:i * P + P], xh3[:, i, :], id_sb[:, :])
                        ins.then_inc(xh3t_ready, 1)

            body(-1, 1, -1, False, True, True)
            with pe.Fori(0, (U - B) // 2) as v:
                for par in range(2):
                    body(v * 2 + par, par, v, True, True, True)
            with pe.Fori((U - B) // 2, U // 2 - 1) as v:
                for par in range(2):
                    body(v * 2 + par, par, v, True, True, False)
            body(U - 2, 0, U // 2 - 1, True, True, False)
            body(U - 1, 1, U // 2 - 1, True, False, False)

            pe.wait_ge(net_loaded, 7 * 16)
            pe.wait_ge(ht_ready, U + B)
            pe.wait_ge(res_ready, U * NT)
            def net_pair(v):
                for par in range(2):
                    b = v * 2 + par
                    yt = hs[:, bass.ds(b, 1), :, :].rearrange("p a t e -> p (a t e)")
                    for c in range(CH):
                        wait_later(pe, g_hid, v * (2 * CH) + max(par * CH + c - 1, 0))
                        nc.tensor.matmul(banks[2 + c % 2][:, :], fw1_sb[:, c * P:c * P + P], yt, start=True, stop=True) \
                            .then_inc(g_mm, 1)
                        nc.tensor.matmul(banks[4 + c % 2][:, :], fw2_sb[:, c * P:c * P + P], yt, start=True, stop=True) \
                            .then_inc(g_mm, 1)
                for stage, (w, src, done) in enumerate(((fh1_sb, hid, g_a), (fh2_sb, hid2, g_b))):
                    for par in range(2):
                        b = v * 2 + par
                        if stage == 0:
                            pe.wait_ge(g_hid, b * CH + CH)
                        else:
                            pe.wait_ge(g_gelu, v * (4 * CH) + par * CH + CH)
                        for c in range(CH):
                            wait_later(pe, g_gelu, v * (4 * CH) + max(stage * 2 * CH + par * CH + c - 1, 0))
                            for k in range(CH):
                                ins = nc.tensor.matmul(banks[c % 2][:, :], w[:, k, c * P:c * P + P], src[par][:, k, :],
                                                       start=(k == 0), stop=(k == CH - 1))
                            ins.then_inc(done, 1)
                for par in range(2):
                    b = v * 2 + par
                    pe.wait_ge(g_gelu, v * (4 * CH) + (3 + par) * CH)
                    wait_later(pe, g_scaled, v * 2)
                    for i in range(NT):
                        for k in range(CH):
                            ins = nc.tensor.matmul(banks[6 + par][:, i * E:i * E + E], hid[par][:, k, i * P:i * P + P],
                                                   fw3_sb[:, k, :], start=(k == 0), stop=(k == CH - 1))
                    ins.then_inc(g_out, 1)

            net_pair(0)
            with pe.Fori(1, B // 2) as v:
                net_pair(v)


def kernel(**inputs):
    import numpy as np
    import concourse.bacc as bacc
    from concourse.bass_utils import run_bass_kernel_spmd

    a = {k.removeprefix("L0_"): np.asarray(v) for k, v in inputs.items()}

    def tokens(z):
        return z.reshape(B, NT, P, E).transpose(0, 2, 1, 3)

    def chunks(w):
        return w.T.reshape(-1, P, w.shape[0]).transpose(1, 0, 2)

    def split_col(v):
        return v.reshape(-1, P).T

    wqk = np.stack([a["attn_Wq"].transpose(0, 2, 1), a["attn_Wk"].transpose(0, 2, 1)], axis=2)
    bqk = np.stack([a["attn_bq"], a["attn_bk"]], axis=2)
    cols = np.stack([np.concatenate([split_col(a["attn_b1"][n]), a["attn_b2"][n][:, None],
                                     a["attn_ln2_w"][n][:, None], a["attn_ln2_b"][n][:, None],
                                     a["attn_ln3_w"][n][:, None], a["attn_ln3_b"][n][:, None]], axis=1) for n in range(D)])
    rows = np.stack([a["attn_ln1_w"], a["attn_ln1_b"], a["attn_ln3_w"], a["attn_ln3_b"]], axis=1)
    pos = np.arange(S)
    rel = np.exp(-np.abs(pos[:, None] - pos[None, :]).astype(np.float64) / 16.0)
    gmat = np.exp(rel).astype(np.float32).reshape(NT, P, NT, P).transpose(3, 0, 2, 1)
    sel = np.tile(np.eye(QS, dtype=np.float32) / H, (HG, 1))
    arrays = {
        "x": tokens(a["attn_x"]), "wqk": wqk, "bqk": bqk,
        "w1t": a["attn_W1"].transpose(0, 2, 1),
        "w2t": np.stack([chunks(a["attn_W2"][n]) for n in range(D)]),
        "cols": cols, "rows": rows,
        "fw1": a["ffn_w1_w"].T, "fw2": a["ffn_w2_w"].T, "fh1": chunks(a["ffn_h1_w"]), "fh2": chunks(a["ffn_h2_w"]),
        "fw3": chunks(a["ffn_w3_w"]),
        "fcols": np.stack([split_col(a[f"ffn_{n}_s"]) for n in ("w1", "w2", "h1", "h2")], axis=1),
        "frow": a["ffn_w3_s"][None, :],
        "gmat": gmat, "sel": sel, "ident": np.eye(P, dtype=np.float32),
    }
    arrays = {k: np.ascontiguousarray(v) for k, v in arrays.items()}
    nc = bacc.Bacc("TRN2", target_bir_lowering=False, num_devices=1)
    aps = [nc.dram_tensor(k, v.shape, mybir.dt.from_np(v.dtype), kind="ExternalInput").ap() for k, v in arrays.items()]
    out = nc.dram_tensor("out", (B, P, NT, E), mybir.dt.float32, kind="ExternalOutput").ap()
    build(nc, *aps, out)
    r = run_bass_kernel_spmd(nc, [arrays], core_ids=[0])
    return np.asarray(r.results[0]["out"]).reshape(B, P, NT, E).transpose(0, 2, 1, 3).reshape(B, S, E)
```

```python
import concourse.bass as bass
from concourse import mybir
from contextlib import ExitStack

D, B, S, E, H, F = 6, 8, 512, 128, 16, 512
DH = E // H
P = 128
NT = S // P
NG = 4
HG = H // NG
QS = P // HG
NQ = NT * NG
TILES = NQ * 4
U = D * B
CH = F // P
EPS = 1e-5
NS = 5
ET = 16
LOADS = 3 + 3 * HG
C_B1, C_B2, C_W2, C_BB2, C_W3, C_BB3 = 0, 4, 5, 6, 7, 8
NCOL = 9


def build(nc, x, wqk, bqk, w1t, w2t, cols, rows, fw1, fw2, fh1, fh2, fw3, fcols, frow, gmat, sel, ident, out):
    f32, f32r = mybir.dt.float32, mybir.dt.float32r
    ALU, ACT, AX = mybir.AluOpType, mybir.ActivationFunctionType, mybir.AxisListType.X
    ctx = ExitStack()
    with ctx:
        def sb(name, shape, dt=f32):
            return ctx.enter_context(nc.sbuf_tensor(name, shape, dt))

        def sem(name):
            return ctx.enter_context(nc.semaphore(name))

        qk_dram = nc.dram_tensor("qk_split", [B, 4, P, S], f32, kind="Internal").ap()

        y_dram = nc.dram_tensor("y_kept", [B, P, NT, E], f32, kind="Internal").ap()

        hc = [sb(f"hc{i}", [P, NT, E + 1]) for i in range(2)]
        hs = sb("hs", [P, B, NT, E])
        ex = sb("ex", [P, ET, S])
        negmax = sb("negmax", [P, ET])
        zsum = sb("zsum", [P, ET])
        zinv = sb("zinv", [P, ET])
        rw = sb("rw", [P, ET, QS])
        ew = sb("ew", [P, 2, S])
        pt = sb("pt", [P, 2, NT, P])
        g_sb = sb("g_sb", [P, NT, NT, P])
        sel_sb = sb("sel_sb", [P, QS])
        id_sb = sb("id_sb", [P, P])
        z2inv = sb("z2inv", [P, NT])
        turn = sb("turn", [P, 1])
        one = sb("one", [P, 1])
        res = sb("res", [P, NT, E])
        bn = sb("bn", [P, 4, NT, 6])
        mv = sb("mv", [P, 4, NT, 2])
        veps = sb("veps", [P, 4, NT])
        rstd = sb("rstd", [P, 4, NT])
        nhalf = sb("nhalf", [P, NT])
        xh1 = sb("xh1", [P, NT, E])
        aff = sb("aff", [P, NT, E])
        xh2 = sb("xh2", [P, NT, E])
        h2t = sb("h2t", [P, S])
        h2r = sb("h2r", [P, S])
        relu = sb("relu", [P, CH, S])
        xh3 = sb("xh3", [P, NT, E])
        h3 = sb("h3", [P, NT, E])
        qf = sb("qf", [P, S])
        kf = sb("kf", [P, S])
        qhi, qlo = sb("qhi", [P, S], f32r), sb("qlo", [P, S], f32r)
        khi, klo = sb("khi", [P, S], f32r), sb("klo", [P, S], f32r)
        xin = [sb(f"xin{i}", [P, NT, E]) for i in range(2)]
        wqk_sb = sb("wqk_sb", [P, 2, E])
        bqk_sb = sb("bqk_sb", [P, 2])
        w1_sb = sb("w1_sb", [P, F])
        w2_sb = sb("w2_sb", [P, CH, E])
        col = sb("col", [P, NCOL])
        row = sb("row", [P, 4, E])
        att = ctx.enter_context(ExitStack())

        def att_sb(name, shape, dt=f32):
            return att.enter_context(nc.sbuf_tensor(name, shape, dt))

        qb = [att_sb(f"qb{i}", [96, NG, HG, S], f32r) for i in range(2)]
        kb = [att_sb(f"kb{i}", [96, NG, S], f32r) for i in range(2)]
        att.close()
        gate = [sb(f"gate{i}", [P, CH, S]) for i in range(2)]
        hid = [sb(f"hid{i}", [P, CH, S]) for i in range(2)]
        hid2 = [sb(f"hid_b{i}", [P, CH, S]) for i in range(2)]
        fh1_sb, fh2_sb = sb("fh1_sb", [P, CH, F]), sb("fh2_sb", [P, CH, F])
        fw1_sb, fw2_sb = sb("fw1_sb", [P, F]), sb("fw2_sb", [P, F])
        fw3_sb = sb("fw3_sb", [P, CH, E])
        fcol = sb("fcol", [P, 4, CH])
        frow_sb = sb("frow_sb", [P, E])
        y_sb = [sb(f"y{i}", [P, NT, E]) for i in range(2)]

        sc = [ctx.enter_context(nc.psum_tensor(f"sc{i}", [P, S], f32)) for i in range(NS)]
        mean = ctx.enter_context(nc.psum_tensor("mean", [P, S], f32))
        m0 = ctx.enter_context(nc.psum_tensor("m0", [P, S], f32))
        m1 = ctx.enter_context(nc.psum_tensor("m1", [P, S], f32))
        up_bank = [m1, m1, m1, m0]
        banks = [*sc, mean, m0, m1]

        const_loaded = sem("const_loaded")
        qkw_loaded = sem("qkw_loaded")
        filled = sem("filled")
        x_loaded = [sem(f"x_loaded{i}") for i in range(2)]
        row_loaded = sem("row_loaded")
        layer_loaded = sem("layer_loaded")
        next_loaded = sem("next_loaded")
        net_loaded = sem("net_loaded")
        qk_loaded = [sem(f"qk_loaded{i}") for i in range(2)]
        hc_loaded = [sem(f"hc_loaded{i}") for i in range(2)]
        kept = sem("kept")
        scores_ready = sem("scores_ready")
        max_ready = sem("max_ready")
        exp_ready = sem("exp_ready")
        zinv_ready = sem("zinv_ready")
        weights_ready = sem("weights_ready")
        summed = sem("summed")
        ew_ready = sem("ew_ready")
        ewt_ready = sem("ewt_ready")
        pt_ready = sem("pt_ready")
        sa_ready = sem("sa_ready")
        z2_ready = sem("z2_ready")
        res_ready = sem("res_ready")
        bn_ready = [sem(f"bn_ready{i}") for i in range(4)]
        mv_ready = [sem(f"mv_ready{i}") for i in range(4)]
        veps_ready = [sem(f"veps_ready{i}") for i in range(4)]
        rstd_ready = [sem(f"rstd_ready{i}") for i in range(4)]
        xh_ready = [sem(f"xh_ready{i}") for i in range(4)]
        h1a_ready, h1_ready = sem("h1a_ready"), sem("h1_ready")
        xh2t_ready = sem("xh2t_ready")
        h2t_ready, h2r_ready = sem("h2t_ready"), sem("h2r_ready")
        up_ready, relu_ready = sem("up_ready"), sem("relu_ready")
        down_ready = sem("down_ready")
        h3a_ready, h3_ready = sem("h3a_ready"), sem("h3_ready")
        xh3t_ready, ht_ready = sem("xh3t_ready"), sem("ht_ready")
        q_ready, k_ready = sem("q_ready"), sem("k_ready")
        qf_ready, kf_ready = sem("qf_ready"), sem("kf_ready")
        qhi_ready, khi_ready = sem("qhi_ready"), sem("khi_ready")
        split_ready = sem("split_ready")
        y_ready = sem("y_ready")
        g_mm, g_silu, g_hid = sem("g_mm"), sem("g_silu"), sem("g_hid")
        g_a, g_b = sem("g_a"), sem("g_b")
        g_gelu = sem("g_gelu")
        g_out, g_scaled, g_done = sem("g_out"), sem("g_scaled"), sem("g_done")
        y_loaded = [sem(f"y_loaded{i}") for i in range(2)]
        stored = sem("stored")

        def bank_user(j):
            if j >= NS:
                return j - NS
            last = [n for n in range(TILES) if n % NS == j][-1]
            return last - TILES

        def permuted(q):
            return q[:, :].rearrange("p (k i n) -> p i n k", i=NT, n=4)

        def by_tile(q):
            return q[:, :].rearrange("p (i n k) -> p i n k", i=NT, n=4)

        def wait_later(engine, what, count):
            if type(count) is not int or count > 0:
                engine.wait_ge(what, count)

        def turns(fori, body):
            body(-1, 1, -1, scores=True, tail=False, late=None)
            body(0, 0, 0, scores=True, tail=True, late=None)
            body(1, 1, 0, scores=True, tail=True, late="inner")
            with fori(1, (U - B) // 2) as v:
                for par in range(2):
                    body(v * 2 + par, par, v, scores=True, tail=True, late="inner")
            v = (U - B) // 2
            body(U - B, 0, v, scores=True, tail=True, late="inner")
            body(U - B + 1, 1, v, scores=True, tail=True, late="last")
            with fori(v + 1, U // 2 - 1) as v:
                for par in range(2):
                    body(v * 2 + par, par, v, scores=True, tail=True, late="last")
            body(U - 2, 0, U // 2 - 1, scores=True, tail=True, late="last")
            body(U - 1, 1, U // 2 - 1, scores=False, tail=True, late="last")
            body(U, 0, U // 2, scores=False, tail=False, late="last")

        block = ctx.enter_context(nc.Block())

        @block.sync
        def _(sp):
            sp.dma_start(wqk_sb[:, :, :], wqk[0]).then_inc(qkw_loaded, 16)
            sp.dma_start(bqk_sb[:, :], bqk[0]).then_inc(qkw_loaded, 16)
            sp.dma_start(id_sb[:, :], ident).then_inc(const_loaded, 16)
            sp.dma_start(g_sb[:, :, :, :], gmat).then_inc(const_loaded, 16)
            sp.dma_start(sel_sb[:, :], sel).then_inc(const_loaded, 16)

            def load_x(b, n, par):
                sp.dma_start(xin[par][:, :, :], x[bass.ds(b, 1), :, :, :].rearrange("a p t e -> p (a t) e")) \
                    .then_inc(x_loaded[par], 16)

            def store_split(b):
                for n, part in enumerate((qhi, qlo, khi, klo)):
                    sp.dma_start(qk_dram[bass.ds(b, 1), n, :, :].rearrange("a p s -> (a p) s"),
                                 part[:, :].bitcast(f32)).then_inc(kept, 16)

            def load_split(b, par):
                for part, src in enumerate((2, 3, 2)):
                    sp.dma_start(kb[par][32 * part:32 * part + 32, :, :].bitcast(f32),
                                 qk_dram[bass.ds(b, 1), src, :, :].rearrange("a (g r) s -> r (a g) s", g=NG)) \
                        .then_inc(qk_loaded[par], 16)
                for part, src in enumerate((0, 0, 1)):
                    for h in range(HG):
                        r = 32 * part + DH * h
                        sp.dma_start(qb[par][r:r + DH, :, h, :].bitcast(f32),
                                     qk_dram[bass.ds(b, 1), src, :, :]
                                     .rearrange("a (g h r) s -> h r (a g) s", g=NG, h=HG)[h]) \
                            .then_inc(qk_loaded[par], 16)

            def load_tokens(b, par):
                sp.dma_start(hc[par][:, :, 0:E], hs[:, bass.ds(b, 1), :, :].rearrange("p a t e -> p (a t) e")) \
                    .then_inc(hc_loaded[par], 16)

            for b in range(2):
                load_x(b, 0, b)
            def first_pair(v):
                for par in range(2):
                    b = v * 2 + par
                    sp.wait_ge(xh_ready[3], b + 1)
                    load_x((b + 2) % B, 0, par)
                    sp.wait_ge(split_ready, b * 2 + 2)
                    store_split(b)

            first_pair(0)
            with sp.Fori(1, B // 2) as v:
                first_pair(v)
            sp.wait_ge(kept, 64 * B)
            sp.wait_ge(filled, 4)
            sp.wait_ge(h3_ready, B)
            for t in range(2):
                load_split(t, t)
                load_tokens(t, t)

            def load_layer(n, first):
                one = bass.ds(n, 1)
                if not first:
                    sp.wait_ge(h3_ready, n * B + B)
                sp.dma_start(row[:, :, :], rows[one, :, :].to_broadcast([P, 4, E])).then_inc(row_loaded, 16)
                if not first:
                    sp.wait_ge(down_ready, n * B)
                    sp.wait_ge(ht_ready, n * B + B)
                sp.dma_start(w1_sb[:, :], w1t[one, :, :].rearrange("a p f -> p (a f)")).then_inc(layer_loaded, 16)
                sp.dma_start(w2_sb[:, :, :], w2t[one, :, :, :].rearrange("a p c e -> p (a c) e")).then_inc(layer_loaded, 16)
                sp.dma_start(col[:, :], cols[one, :, :].rearrange("a p c -> p (a c)")).then_inc(layer_loaded, 16)

            def load_next(n):
                sp.wait_ge(kf_ready, n * B + B)
                sp.wait_ge(qf_ready, n * B + B)
                nxt = bass.ds(n + 1, 1)
                sp.dma_start(wqk_sb[:, :, :], wqk[nxt, :, :, :].rearrange("a p c e -> p (a c) e")).then_inc(next_loaded, 16)
                sp.dma_start(bqk_sb[:, :], bqk[nxt, :, :].rearrange("a p c -> p (a c)")).then_inc(next_loaded, 16)

            def load_x_again(u, par):
                sp.dma_start(xin[par][:, :, :], x[bass.ds(u % B, 1), :, :, :].rearrange("a p t e -> p (a t) e")) \
                    .then_inc(x_loaded[par], 16)

            def body(u, par, late, layer=None, more=True, again=True):
                w = u - 1
                if more:
                    sp.wait_ge(scores_ready, u * TILES + TILES)
                    load_split((u + 2) % B, par)
                if layer is not None:
                    load_layer(layer, late is None)
                if more:
                    sp.wait_ge(res_ready, u * NT + NT)
                    load_tokens((u + 2) % B, par)
                if late == "inner":
                    sp.wait_ge(split_ready, w * 2 + 2 * B + 2)
                    store_split(w % B)
                if late == "last":
                    sp.wait_ge(y_ready, w - (U - B) + 1)
                    sp.dma_start(y_dram[bass.ds(w % B, 1), :, :, :].rearrange("a p t e -> p (a t) e"), h3[:, :, :]) \
                        .then_inc(kept, 16)
                    if again:
                        load_x_again(w + 2, 1 - par)

            load_layer(0, True)
            load_next(0)
            body(0, 0, None)
            body(1, 1, "inner")
            with sp.Fori(1, B // 2) as v:
                for par in range(2):
                    body(v * 2 + par, par, "inner")
            with sp.Fori(1, D - 1) as n:
                body(n * B, 0, "inner", layer=n)
                load_next(n)
                body(n * B + 1, 1, "inner")
                with sp.Fori(1, B // 2) as v:
                    for par in range(2):
                        body(n * B + v * 2 + par, par, "inner")
            body(U - B, 0, "inner", layer=D - 1)
            sp.wait_ge(kept, U * 64)
            body(U - B + 1, 1, "last")
            with sp.Fori(1, B // 2 - 1) as v:
                for par in range(2):
                    body(v * 2 + (U - B) + par, par, "last")
            sp.wait_ge(scores_ready, U * TILES)
            for dst, src in ((fw1_sb[:, :], fw1), (fw2_sb[:, :], fw2), (fh1_sb[:, :, :], fh1), (fh2_sb[:, :, :], fh2),
                             (fw3_sb[:, :, :], fw3), (fcol[:, :, :], fcols), (frow_sb[:, :], frow.to_broadcast([P, E]))):
                sp.dma_start(dst, src).then_inc(net_loaded, 16)
            body(U - 2, 0, "last", more=False)
            body(U - 1, 1, "last", more=False, again=False)
            body(U, 0, "last", more=False, again=False)

            def load_y(b, par):
                sp.dma_start(y_sb[par][:, :, :], y_dram[bass.ds(b, 1), :, :, :].rearrange("a p t e -> p (a t) e")) \
                    .then_inc(y_loaded[par], 16)

            sp.wait_ge(kept, 64 * U + 16 * B)
            load_y(0, 0)
            load_y(1, 1)
            def net_pair(v):
                for par in range(2):
                    b = v * 2 + par
                    sp.wait_ge(g_done, b + 1)
                    sp.dma_start(out[bass.ds(b, 1), :, :, :].rearrange("a p t e -> p (a t) e"), y_sb[par][:, :, :]) \
                        .then_inc(stored, 16)
                    sp.wait_ge(stored, b * 16 + 16)
                    load_y((b + 2) % B, par)

            net_pair(0)
            with sp.Fori(1, B // 2) as v:
                net_pair(v)
            for par in range(2):
                sp.wait_ge(y_loaded[par], 16 * (B // 2 + 1))

        @block.gpsimd
        def _(gp):
            gp.memset(one[:, :], 1.0)
            gp.memset(nhalf[:, :], -0.5).then_inc(filled, 1)
            for i in range(2):
                gp.memset(hc[i][:, :, E:E + 1], 1.0)
                gp.memset(qb[i][:, :, :, :].bitcast(f32), 0.0).then_inc(filled, 1)
            gp.memset(negmax[:, :], 0.0).then_inc(filled, 1)
            gp.wait_ge(filled, 4)

            def power(k, n):
                gp.wait_ge(veps_ready[k], n)
                nc.gpsimd.tensor_tensor(rstd[:, k, :], veps[:, k, :], nhalf[:, :], ALU.pow).then_inc(rstd_ready[k], 1)

            def low_part(full, high, low, full_ready, high_ready, n):
                gp.wait_ge(full_ready, n)
                nc.gpsimd.tensor_tensor(high[:, :], full[:, :], one[:, 0:1].to_broadcast([P, S]), ALU.mult) \
                    .then_inc(high_ready, 1)
                gp.wait_ge(high_ready, n)
                nc.gpsimd.tensor_tensor(low[:, :], full[:, :], high[:, :].bitcast(f32), ALU.subtract) \
                    .then_inc(split_ready, 1)

            def first_pair(v):
                for par in range(2):
                    b = v * 2 + par
                    power(3, b + 1)
                    gp.wait_ge(xh_ready[3], b + 1)
                    nc.gpsimd.tensor_copy(hs[:, bass.ds(b, 1), :, :].rearrange("p a t e -> p (a t e)"),
                                          xh3[:, :, :].rearrange("p t e -> p (t e)")).then_inc(h3_ready, 1)

            first_pair(0)
            with gp.Fori(1, B // 2) as v:
                first_pair(v)

            def row_weights(t, q):
                gp.wait_ge(zinv_ready, t * NQ + q + 1)
                c = 4 * q % ET
                nc.gpsimd.tensor_tensor(rw[:, c:c + 4, :],
                                        sel_sb[:, :].rearrange("p (a q) -> p a q", a=1).to_broadcast([P, 4, QS]),
                                        zinv[:, c:c + 4].rearrange("p (a q) -> p a q", q=1).to_broadcast([P, 4, QS]),
                                        ALU.mult).then_inc(weights_ready, 1)

            def high_part(full, high, full_ready, high_ready, n):
                gp.wait_ge(full_ready, n)
                nc.gpsimd.tensor_tensor(high[:, :], full[:, :], one[:, 0:1].to_broadcast([P, S]), ALU.mult) \
                    .then_inc(high_ready, 1)

            def low_part(full, high, low, high_ready, n):
                gp.wait_ge(high_ready, n)
                nc.gpsimd.tensor_tensor(low[:, :], full[:, :], high[:, :].bitcast(f32), ALU.subtract) \
                    .then_inc(split_ready, 1)

            gp.wait_ge(const_loaded, 48)

            def body(u, par, v, scores, tail, late):
                t, w = u + 1, u - 1
                y = w - (U - B)
                inner, last = late == "inner", late == "last"
                if tail:
                    row_weights(u, NQ - 1)
                if scores:
                    row_weights(t, 0)
                    row_weights(t, 1)
                if late:
                    power(2, w + 1)
                if scores:
                    row_weights(t, 2)
                if late:
                    gp.wait_ge(xh_ready[2], w + 1)
                    nc.gpsimd.tensor_tensor(aff[:, :, :], xh3[:, :, :], row[:, 2:3, :].to_broadcast([P, NT, E]), ALU.mult) \
                        .then_inc(h3a_ready, 1)
                if inner:
                    gp.wait_ge(h3a_ready, w + 1)
                    nc.gpsimd.tensor_tensor(hs[:, bass.ds(w % B, 1), :, :].rearrange("p a t e -> p (a t) e"),
                                            aff[:, :, :], row[:, 3:4, :].to_broadcast([P, NT, E]), ALU.add) \
                        .then_inc(h3_ready, 1)
                if last:
                    gp.wait_ge(h3a_ready, w + 1)
                    nc.gpsimd.tensor_tensor(aff[:, :, :], aff[:, :, :], row[:, 3:4, :].to_broadcast([P, NT, E]), ALU.add) \
                        .then_inc(h3_ready, 1)
                    gp.wait_ge(h3_ready, w + B + 1)
                    gp.wait_ge(x_loaded[1 - par], (y // 2) * 16 + (B // 2 + 1) * 16)
                    wait_later(gp, kept, y * 16 + 64 * U)
                    nc.gpsimd.tensor_tensor(h3[:, :, :], aff[:, :, :], xin[1 - par][:, :, :], ALU.add).then_inc(y_ready, 1)
                if scores:
                    row_weights(t, 3)
                if tail:
                    gp.wait_ge(row_loaded, (u // B) * 16 + 16)
                    power(0, u + 1)
                if scores:
                    row_weights(t, 4)
                if tail:
                    gp.wait_ge(xh_ready[0], u + 1)
                    nc.gpsimd.tensor_tensor(aff[:, :, :], xh1[:, :, :], row[:, 0:1, :].to_broadcast([P, NT, E]), ALU.mult) \
                        .then_inc(h1a_ready, 1)
                if scores:
                    row_weights(t, 5)
                if tail:
                    gp.wait_ge(h1a_ready, u + 1)
                    nc.gpsimd.tensor_tensor(aff[:, :, :], aff[:, :, :], row[:, 1:2, :].to_broadcast([P, NT, E]), ALU.add) \
                        .then_inc(h1_ready, 1)
                if last:
                    power(3, y + B + 1)
                if scores:
                    row_weights(t, 6)
                if tail:
                    power(1, u + 1)
                if scores:
                    row_weights(t, 7)
                if inner:
                    gp.wait_ge(kept, w * 64 + 64 * B)
                    high_part(qf, qhi, qf_ready, qhi_ready, w + B + 1)
                    low_part(qf, qhi, qlo, qhi_ready, w + B + 1)
                if scores:
                    row_weights(t, 8)
                if tail:
                    gp.wait_ge(layer_loaded, (u // B) * 48 + 48)
                    gp.wait_ge(h2t_ready, u + 1)
                    nc.gpsimd.tensor_tensor(h2r[:, :], h2t[:, :], col[:, C_B2:C_B2 + 1].to_broadcast([P, S]), ALU.add) \
                        .then_inc(h2r_ready, 1)
                if scores:
                    row_weights(t, 9)
                if inner:
                    high_part(kf, khi, kf_ready, khi_ready, w + B + 1)
                if scores:
                    row_weights(t, 10)
                if inner:
                    low_part(kf, khi, klo, khi_ready, w + B + 1)
                if scores:
                    for q in range(11, NQ - 1):
                        row_weights(t, q)

            turns(gp.Fori, body)

        @block.vector
        def _(dve):
            def split(full, high, low, full_ready, high_ready, n):
                dve.wait_ge(full_ready, n)
                nc.vector.tensor_copy(high[:, :], full[:, :]).then_inc(high_ready, 1)
                dve.wait_ge(high_ready, n)
                nc.vector.tensor_tensor(low[:, :], full[:, :], high[:, :].bitcast(f32), ALU.subtract) \
                    .then_inc(split_ready, 1)

            def stats(src, k, i, src_ready, n, last):
                dve.wait_ge(src_ready, n)
                ins = nc.vector.bn_stats(bn[:, k, i, :], src)
                if last:
                    ins.then_inc(bn_ready[k], 1)

            def spread(k, n):
                for i in range(NT):
                    ins = nc.vector.bn_aggr(mv[:, k, i, :], bn[:, k, i, :])
                ins.then_inc(mv_ready[k], 1)
                dve.wait_ge(mv_ready[k], n)
                nc.vector.tensor_scalar(veps[:, k, :], mv[:, k, :, 1], EPS, None, ALU.add).then_inc(veps_ready[k], 1)

            def apply(dst, src, k, n):
                dve.wait_ge(rstd_ready[k], n)
                for i in range(NT):
                    ins = nc.vector.tensor_scalar(dst[:, i, :], src(i), mv[:, k, i, 0:1], rstd[:, k, i:i + 1],
                                                  ALU.subtract, ALU.mult)
                ins.then_inc(xh_ready[k], 1)

            dve.wait_ge(qkw_loaded, 32)
            dve.wait_ge(filled, 4)
            def first_pair(v):
                for par in range(2):
                    b = v * 2 + par
                    for i in range(NT):
                        stats(xin[par][:, i, :], 3, i, x_loaded[par], v * 16 + 16, i == NT - 1)
                    dve.wait_ge(bn_ready[3], b + 1)
                    nc.vector.memset(turn[:, :], 0.0)
                    spread(3, b + 1)
                    wait_later(dve, h3_ready, b)
                    wait_later(dve, xh3t_ready, b)
                    apply(xh3, lambda i: xin[par][:, i, :], 3, b + 1)
                    dve.wait_ge(q_ready, b + 1)
                    nc.vector.tensor_scalar(permuted(qf), by_tile(m0), bqk_sb[:, 0:1], DH ** -0.5, ALU.add, ALU.mult) \
                        .then_inc(qf_ready, 1)
                    wait_later(dve, kept, b * 64)
                    split(qf, qhi, qlo, qf_ready, qhi_ready, b + 1)
                    split(kf, khi, klo, kf_ready, khi_ready, b + 1)

            first_pair(0)
            with dve.Fori(1, B // 2) as v:
                first_pair(v)

            def score_max(t, j):
                dve.wait_ge(scores_ready, t * TILES + j + 1)
                nc.vector.tensor_reduce(negmax[:, j % ET:j % ET + 1], sc[j % NS][:, :], AX, ALU.max, negate=True) \
                    .then_inc(max_ready, 1)

            def invert_sums(t, q):
                dve.wait_ge(exp_ready, t * TILES + 4 * q + 4)
                c = 4 * q % ET
                nc.vector.reciprocal(zinv[:, c:c + 4], zsum[:, c:c + 4]).then_inc(zinv_ready, 1)

            def relative(t, i):
                dve.wait_ge(ewt_ready, t * NT + i + 1)
                nc.vector.tensor_tensor(pt[:, i % 2, :, :], m0[:, :].rearrange("p (c l) -> p c l", c=NT),
                                        g_sb[:, i, :, :], ALU.mult).then_inc(pt_ready, 1)

            def invert_row(t, i):
                dve.wait_ge(sa_ready, t * NT + i + 1)
                nc.vector.reciprocal(z2inv[:, i:i + 1], m0[:, E:E + 1]).then_inc(z2_ready, 1)

            def residual(t, i, par):
                dve.wait_ge(z2_ready, t * NT + i + 1)
                nc.vector.scalar_tensor_tensor(res[:, i, :], m0[:, 0:E], z2inv[:, i:i + 1],
                                               hc[par][:, i, 0:E], ALU.mult, ALU.add).then_inc(res_ready, 1)

            def body(u, par, v, scores, tail, late):
                t, tp, w = u + 1, 1 - par, u - 1
                y = w - (U - B) + B
                inner, last = late == "inner", late == "last"
                for j in range(TILES):
                    if tail and j == 20:
                        dve.wait_ge(bn_ready[0], u + 1)
                    if tail and j == 31:
                        dve.wait_ge(bn_ready[1], u + 1)
                    if late and j == 11:
                        dve.wait_ge(bn_ready[2], w + 1)
                    if last and j == 22:
                        dve.wait_ge(bn_ready[3], y + 1)
                    if scores:
                        score_max(t, j)
                    if j == 1 and tail:
                        invert_sums(u, NQ - 1)
                    if j % 4 == 1 and j > 4 and scores:
                        invert_sums(t, j // 4 - 1)
                    for i, at, n, on, pn in ((2, 1, u, tail, par), (3, 17, u, tail, par),
                                             (0, 33, t, scores, tp), (1, 49, t, scores, tp)):
                        if on and j == at:
                            invert_row(n, i)
                        if on and j == at + 1:
                            residual(n, i, pn)
                        if on and j == at + 2:
                            stats(res[:, i, :], 0, i, res_ready, n * NT + i + 1, i == NT - 1)
                    for i, at, n, on in ((3, 12, u, tail), (0, 28, t, scores), (1, 44, t, scores), (2, 60, t, scores)):
                        if on and j == at:
                            relative(n, i)
                    if late and j == 10:
                        for i in range(NT):
                            stats(m1[:, i * E:i * E + E], 2, i, down_ready, w + 1, i == NT - 1)
                    if late and j == 11:
                        spread(2, w + 1)
                    if late and j == 14:
                        apply(xh3, lambda i: m1[:, i * E:i * E + E], 2, w + 1)
                    if tail and j == 20:
                        spread(0, u + 1)
                    if last and j == 21:
                        for i in range(NT):
                            stats(h3[:, i, :], 3, i, y_ready, y - B + 1, i == NT - 1)
                    if last and j == 22:
                        spread(3, y + 1)
                    if tail and j == 23:
                        apply(xh1, lambda i: res[:, i, :], 0, u + 1)
                    if inner and j == 24:
                        dve.wait_ge(q_ready, w + B + 1)
                        nc.vector.tensor_scalar(permuted(qf), by_tile(m1), bqk_sb[:, 0:1], DH ** -0.5, ALU.add, ALU.mult) \
                            .then_inc(qf_ready, 1)
                    if tail and j == 30:
                        for i in range(NT):
                            stats(aff[:, i, :], 1, i, h1_ready, u + 1, i == NT - 1)
                    if tail and j == 31:
                        spread(1, u + 1)
                    if last and j == 32:
                        apply(xh3, lambda i: h3[:, i, :], 3, y + 1)
                    if tail and j == 34:
                        apply(xh2, lambda i: aff[:, i, :], 1, u + 1)

            turns(dve.Fori, body)

            dve.wait_ge(net_loaded, 7 * 16)
            def net_pair(v):
                for par in range(2):
                    b = v * 2 + par
                    for c in range(CH):
                        dve.wait_ge(g_silu, b * CH + c + 1)
                        nc.vector.scalar_tensor_tensor(hid[par][:, c, :], banks[4 + c % 2][:, :], fcol[:, 1, c:c + 1],
                                                       gate[par][:, c, :], ALU.mult, ALU.mult).then_inc(g_hid, 1)
                for par in range(2):
                    b = v * 2 + par
                    dve.wait_ge(g_out, b + 1)
                    nc.vector.tensor_tensor(gate[par][:, :, 0:E], banks[6 + par][:, :].rearrange("p (t e) -> p t e", t=NT),
                                            frow_sb[:, :].rearrange("p (a e) -> p a e", a=1).to_broadcast([P, NT, E]),
                                            ALU.mult).then_inc(g_scaled, 1)
                    dve.wait_ge(g_scaled, b + 1)
                    dve.wait_ge(y_loaded[par], v * 16 + 16)
                    nc.vector.tensor_tensor(y_sb[par][:, :, :], y_sb[par][:, :, :], gate[par][:, :, 0:E], ALU.add) \
                        .then_inc(g_done, 1)

            net_pair(0)
            with dve.Fori(1, B // 2) as v:
                net_pair(v)

        @block.scalar
        def _(act):
            act.wait_ge(qkw_loaded, 32)
            def first_pair(v):
                for par in range(2):
                    b = v * 2 + par
                    act.wait_ge(xh3t_ready, b + 1)
                    nc.scalar.activation(h2t[:, :], m1[:, :], ACT.Copy).then_inc(ht_ready, 1)
                    act.wait_ge(k_ready, b + 1)
                    wait_later(act, split_ready, b * 2)
                    nc.scalar.activation(kf[:, :], mean[:, :], ACT.Identity, bias=bqk_sb[:, 1:2]).then_inc(kf_ready, 1)

            first_pair(0)
            with act.Fori(1, B // 2) as v:
                first_pair(v)

            def exp_scores(t, j):
                act.wait_ge(max_ready, t * TILES + j + 1)
                if j % 4 == 0 and (type(t) is not int or t > 0 or j >= ET):
                    act.wait_ge(summed, t * NQ + j // 4 - 3)
                c = j % ET
                nc.scalar.activation(ex[:, c, :], sc[j % NS][:, :], ACT.Exp, bias=negmax[:, c:c + 1],
                                     accum_out=zsum[:, c:c + 1]).then_inc(exp_ready, 1)

            def exp_mean(t, i):
                act.wait_ge(summed, t * NQ + 4 * i + 4)
                if type(t) is not int or t > 0 or i >= 2:
                    act.wait_ge(ewt_ready, t * NT + i - 1)
                nc.scalar.activation(ew[:, i % 2, :], mean[:, :], ACT.Exp).then_inc(ew_ready, 1)

            def affine(src, k, done):
                nc.scalar.activation(h2t[:, :], src[:, :], ACT.Identity, scale=col[:, k:k + 1], bias=col[:, k + 1:k + 2]) \
                    .then_inc(done, 1)

            def body(u, par, v, scores, tail, late):
                t, w = u + 1, u - 1
                inner, last = late == "inner", late == "last"
                for j in range(TILES):
                    if scores:
                        exp_scores(t, j)
                    if j == 6 and tail:
                        exp_mean(u, 3)
                    if j in (22, 38, 54) and scores:
                        exp_mean(t, j // 16 - 1)
                    if inner and j == 17:
                        act.wait_ge(xh3t_ready, w + B + 1)
                        affine(m1, C_W3, ht_ready)
                    if inner and j == 24:
                        act.wait_ge(k_ready, w + B + 1)
                        act.wait_ge(split_ready, w * 2 + 2 * B)
                        nc.scalar.activation(kf[:, :], m0[:, :], ACT.Identity, bias=bqk_sb[:, 1:2]).then_inc(kf_ready, 1)
                    if last and j == 36:
                        act.wait_ge(xh3t_ready, w - (U - B) + U + 1)
                        nc.scalar.activation(hs[:, bass.ds(w % B, 1), :, :].rearrange("p a t e -> p (a t e)"), m1[:, :],
                                             ACT.Copy).then_inc(ht_ready, 1)
                    if tail and j == 39:
                        act.wait_ge(layer_loaded, (u // B) * 48 + 48)
                        act.wait_ge(xh2t_ready, u + 1)
                        affine(m1, C_W2, h2t_ready)
                    for c, at in ((0, 44), (1, 48), (2, 52), (3, 55)):
                        if tail and j == at:
                            act.wait_ge(up_ready, u * CH + c + 1)
                            nc.scalar.activation(relu[:, c, :], up_bank[c][:, :], ACT.Relu,
                                                 bias=col[:, C_B1 + c:C_B1 + c + 1]).then_inc(relu_ready, 1)

            turns(act.Fori, body)

            act.wait_ge(net_loaded, 7 * 16)
            def net_pair(v):
                for par in range(2):
                    b = v * 2 + par
                    for c in range(CH):
                        act.wait_ge(g_mm, b * 2 * CH + 2 * c + 2)
                        wait_later(act, g_done, v * 2)
                        nc.scalar.activation(gate[par][:, c, :], banks[2 + c % 2][:, :], ACT.Silu,
                                             scale=fcol[:, 0, c:c + 1]).then_inc(g_silu, 1)
                for k, product, dst in ((2, g_a, hid2), (3, g_b, hid)):
                    for par in range(2):
                        b = v * 2 + par
                        for c in range(CH):
                            act.wait_ge(product, b * CH + c + 1)
                            nc.scalar.activation(dst[par][:, c, :], banks[c % 2][:, :], ACT.Gelu,
                                                 scale=fcol[:, k, c:c + 1]).then_inc(g_gelu, 1)

            net_pair(0)
            with act.Fori(1, B // 2) as v:
                net_pair(v)

        @block.tensor
        def _(pe):
            pe.wait_ge(const_loaded, 48)
            pe.wait_ge(qkw_loaded, 32)
            def first_pair(v):
                for par in range(2):
                    b = v * 2 + par
                    pe.wait_ge(xh_ready[3], b + 1)
                    for i in range(NT):
                        ins = nc.tensor.transpose(m1[:, i * P:i * P + P], xh3[:, i, :], id_sb[:, :])
                    ins.then_inc(xh3t_ready, 1)
                    pe.wait_ge(ht_ready, b + 1)
                    wait_later(pe, qf_ready, b)
                    nc.tensor.matmul(m0[:, :], wqk_sb[:, 0, :], h2t[:, :], start=True, stop=True).then_inc(q_ready, 1)
                    wait_later(pe, kf_ready, b)
                    nc.tensor.matmul(mean[:, :], wqk_sb[:, 1, :], h2t[:, :], start=True, stop=True).then_inc(k_ready, 1)

            first_pair(0)
            with pe.Fori(1, B // 2) as v:
                first_pair(v)

            def score_tile(t, j, par):
                q, n = j // 4, j % 4
                i, g = q // NG, q % NG
                free = bank_user(j)
                if type(t) is not int or t > 0 or free >= 0:
                    pe.wait_ge(exp_ready, t * TILES + free + 1)
                flat = qb[par][:, g, :, :].rearrange("r h s -> r (h s)")
                nc.tensor.matmul(sc[j % NS][:, :], flat[:, NT * i + n::S // QS], kb[par][:, g, :], start=True, stop=True) \
                    .then_inc(scores_ready, 1)

            def sum_heads(t, q):
                pe.wait_ge(weights_ready, t * NQ + q + 1)
                i, g = q // NG, q % NG
                if g == 0 and (type(t) is not int or t > 0 or i > 0):
                    pe.wait_ge(ew_ready, t * NT + i)
                for n in range(4):
                    c = (4 * q + n) % ET
                    ins = nc.tensor.matmul(mean[n * QS:(n + 1) * QS, :], rw[:, c, :], ex[:, c, :],
                                           start=(g == 0), stop=(g == NG - 1))
                ins.then_inc(summed, 1)

            def transpose_mean(t, i):
                pe.wait_ge(ew_ready, t * NT + i + 1)
                for c in range(NT):
                    ins = nc.tensor.transpose(m0[:, c * P:c * P + P], ew[:, i % 2, c * P:c * P + P], id_sb[:, :])
                ins.then_inc(ewt_ready, 1)

            def attend(t, i, par, loaded):
                pe.wait_ge(hc_loaded[par], loaded)
                pe.wait_ge(pt_ready, t * NT + i + 1)
                for c in range(NT):
                    ins = nc.tensor.matmul(m0[:, 0:E + 1], pt[:, i % 2, c, :], hc[par][:, c, :],
                                           start=(c == 0), stop=(c == NT - 1))
                ins.then_inc(sa_ready, 1)

            def transpose_tokens(src, done):
                for i in range(NT):
                    ins = nc.tensor.transpose(m1[:, i * P:i * P + P], src[:, i, :], id_sb[:, :])
                ins.then_inc(done, 1)

            def up(c):
                nc.tensor.matmul(up_bank[c][:, :], w1_sb[:, c * P:c * P + P], h2t[:, :], start=True, stop=True) \
                    .then_inc(up_ready, 1)

            def down(i, done):
                dst = m1[:, i * E:i * E + E]
                nc.tensor.matmul(dst, h2r[:, i * P:i * P + P], id_sb[:, :], start=True, stop=False)
                for c in range(CH):
                    ins = nc.tensor.matmul(dst, relu[:, c, i * P:i * P + P], w2_sb[:, c, :], start=False, stop=(c == CH - 1))
                if done is not None:
                    ins.then_inc(done, 1)

            def body(u, par, v, scores, tail, late):
                t, tp, w = u + 1, 1 - par, u - 1
                tv = v + par
                inner, last = late == "inner", late == "last"
                for j in range(TILES):
                    if scores:
                        if j == 0:
                            pe.wait_ge(qk_loaded[tp], tv * (16 * LOADS) + 16 * LOADS)
                        score_tile(t, j, tp)
                    if j in (0, 4, 8) and tail:
                        sum_heads(u, j // 4 + 13)
                    if scores and j % 4 == 0 and j >= 16 and j % 16 != 12:
                        sum_heads(t, j // 4 - 3)
                    if scores and j % 16 == 14:
                        sum_heads(t, j // 4 - 3)
                    if j == 13 and tail:
                        pe.wait_ge(res_ready, u * NT + 3)
                        transpose_mean(u, 3)
                    if j in (29, 45, 61) and scores:
                        i = j // 16 - 1
                        if i == 0 and inner:
                            pe.wait_ge(kf_ready, w + B + 1)
                        if i == 2 and tail:
                            pe.wait_ge(relu_ready, u * CH + 4)
                        if type(t) is not int or t * NT + i > 0:
                            pe.wait_ge(res_ready, t * NT + i)
                        transpose_mean(t, i)
                    if j == 2 and tail:
                        attend(u, 2, par, v * 16 + 16)
                    if j == 18 and tail:
                        attend(u, 3, par, v * 16 + 16)
                    if j in (34, 50) and scores:
                        attend(t, j // 16 - 2, tp, tv * 16 + 16)
                    if late and j in (3, 6, 10):
                        down({3: 1, 6: 2, 10: 3}[j], down_ready if j == 10 else None)
                    if inner and j == 19:
                        pe.wait_ge(xh_ready[2], w + 1)
                        transpose_tokens(xh3, xh3t_ready)
                    if inner and j == 25:
                        pe.wait_ge(ht_ready, w + B + 1)
                        pe.wait_ge(next_loaded, (w // B) * 32 + 32)
                        nc.tensor.matmul(m1[:, :], wqk_sb[:, 0, :], h2t[:, :], start=True, stop=True).then_inc(q_ready, 1)
                    if inner and j == 26:
                        pe.wait_ge(res_ready, u * NT + 4)
                        nc.tensor.matmul(m0[:, :], wqk_sb[:, 1, :], h2t[:, :], start=True, stop=True).then_inc(k_ready, 1)
                    if last and j == 37:
                        pe.wait_ge(xh_ready[3], w - (U - B) + B + 1)
                        transpose_tokens(xh3, xh3t_ready)
                    if tail and j == 41:
                        if inner:
                            pe.wait_ge(qf_ready, w + B + 1)
                        if last:
                            pe.wait_ge(ht_ready, w + B + 1)
                        pe.wait_ge(xh_ready[1], u + 1)
                        transpose_tokens(xh2, xh2t_ready)
                    if tail and j == 47:
                        pe.wait_ge(layer_loaded, (u // B) * 48 + 48)
                        pe.wait_ge(h2t_ready, u + 1)
                        up(0)
                    if tail and j == 51:
                        pe.wait_ge(relu_ready, u * CH + 1)
                        up(1)
                    if tail and j == 55:
                        pe.wait_ge(relu_ready, u * CH + 2)
                        up(2)
                    if tail and j == 57:
                        if scores:
                            pe.wait_ge(res_ready, t * NT + 2)
                        else:
                            pe.wait_ge(res_ready, u * NT + 4)
                        up(3)
                    if tail and j == 63:
                        pe.wait_ge(relu_ready, u * CH + 4)
                        pe.wait_ge(h2r_ready, u + 1)
                        down(0, None)

            turns(pe.Fori, body)

            pe.wait_ge(net_loaded, 7 * 16)
            pe.wait_ge(ht_ready, U + B)
            pe.wait_ge(res_ready, U * NT)
            def net_pair(v):
                for par in range(2):
                    b = v * 2 + par
                    yt = hs[:, bass.ds(b, 1), :, :].rearrange("p a t e -> p (a t e)")
                    for c in range(CH):
                        wait_later(pe, g_hid, v * (2 * CH) + max(par * CH + c - 1, 0))
                        nc.tensor.matmul(banks[2 + c % 2][:, :], fw1_sb[:, c * P:c * P + P], yt, start=True, stop=True) \
                            .then_inc(g_mm, 1)
                        nc.tensor.matmul(banks[4 + c % 2][:, :], fw2_sb[:, c * P:c * P + P], yt, start=True, stop=True) \
                            .then_inc(g_mm, 1)
                for stage, (w, src, done) in enumerate(((fh1_sb, hid, g_a), (fh2_sb, hid2, g_b))):
                    for par in range(2):
                        b = v * 2 + par
                        if stage == 0:
                            pe.wait_ge(g_hid, b * CH + CH)
                        else:
                            pe.wait_ge(g_gelu, v * (4 * CH) + par * CH + CH)
                        for c in range(CH):
                            wait_later(pe, g_gelu, v * (4 * CH) + max(stage * 2 * CH + par * CH + c - 1, 0))
                            for k in range(CH):
                                ins = nc.tensor.matmul(banks[c % 2][:, :], w[:, k, c * P:c * P + P], src[par][:, k, :],
                                                       start=(k == 0), stop=(k == CH - 1))
                            ins.then_inc(done, 1)
                for par in range(2):
                    b = v * 2 + par
                    pe.wait_ge(g_gelu, v * (4 * CH) + (3 + par) * CH)
                    wait_later(pe, g_scaled, v * 2)
                    for i in range(NT):
                        for k in range(CH):
                            ins = nc.tensor.matmul(banks[6 + par][:, i * E:i * E + E], hid[par][:, k, i * P:i * P + P],
                                                   fw3_sb[:, k, :], start=(k == 0), stop=(k == CH - 1))
                    ins.then_inc(g_out, 1)

            net_pair(0)
            with pe.Fori(1, B // 2) as v:
                net_pair(v)


def kernel(**inputs):
    import numpy as np
    import concourse.bacc as bacc
    from concourse.bass_utils import run_bass_kernel_spmd

    a = {k.removeprefix("L0_"): np.asarray(v) for k, v in inputs.items()}

    def tokens(z):
        return z.reshape(B, NT, P, E).transpose(0, 2, 1, 3)

    def chunks(w):
        return w.T.reshape(-1, P, w.shape[0]).transpose(1, 0, 2)

    def split_col(v):
        return v.reshape(-1, P).T

    wqk = np.stack([a["attn_Wq"].transpose(0, 2, 1), a["attn_Wk"].transpose(0, 2, 1)], axis=2)
    bqk = np.stack([a["attn_bq"], a["attn_bk"]], axis=2)
    cols = np.stack([np.concatenate([split_col(a["attn_b1"][n]), a["attn_b2"][n][:, None],
                                     a["attn_ln2_w"][n][:, None], a["attn_ln2_b"][n][:, None],
                                     a["attn_ln3_w"][n][:, None], a["attn_ln3_b"][n][:, None]], axis=1) for n in range(D)])
    rows = np.stack([a["attn_ln1_w"], a["attn_ln1_b"], a["attn_ln3_w"], a["attn_ln3_b"]], axis=1)
    pos = np.arange(S)
    rel = np.exp(-np.abs(pos[:, None] - pos[None, :]).astype(np.float64) / 16.0)
    gmat = np.exp(rel).astype(np.float32).reshape(NT, P, NT, P).transpose(3, 0, 2, 1)
    sel = np.tile(np.eye(QS, dtype=np.float32) / H, (HG, 1))
    arrays = {
        "x": tokens(a["attn_x"]), "wqk": wqk, "bqk": bqk,
        "w1t": a["attn_W1"].transpose(0, 2, 1),
        "w2t": np.stack([chunks(a["attn_W2"][n]) for n in range(D)]),
        "cols": cols, "rows": rows,
        "fw1": a["ffn_w1_w"].T, "fw2": a["ffn_w2_w"].T, "fh1": chunks(a["ffn_h1_w"]), "fh2": chunks(a["ffn_h2_w"]),
        "fw3": chunks(a["ffn_w3_w"]),
        "fcols": np.stack([split_col(a[f"ffn_{n}_s"]) for n in ("w1", "w2", "h1", "h2")], axis=1),
        "frow": a["ffn_w3_s"][None, :],
        "gmat": gmat, "sel": sel, "ident": np.eye(P, dtype=np.float32),
    }
    arrays = {k: np.ascontiguousarray(v) for k, v in arrays.items()}
    nc = bacc.Bacc("TRN2", target_bir_lowering=False, num_devices=1)
    aps = [nc.dram_tensor(k, v.shape, mybir.dt.from_np(v.dtype), kind="ExternalInput").ap() for k, v in arrays.items()]
    out = nc.dram_tensor("out", (B, P, NT, E), mybir.dt.float32, kind="ExternalOutput").ap()
    build(nc, *aps, out)
    r = run_bass_kernel_spmd(nc, [arrays], core_ids=[0])
    return np.asarray(r.results[0]["out"]).reshape(B, P, NT, E).transpose(0, 2, 1, 3).reshape(B, S, E)
```

```python
import concourse.bass as bass
from concourse import mybir
from contextlib import ExitStack

D, B, S, E, H, F = 6, 8, 512, 128, 16, 512
DH = E // H
P = 128
NT = S // P
NG = 4
HG = H // NG
QS = P // HG
NQ = NT * NG
TILES = NQ * 4
U = D * B
CH = F // P
EPS = 1e-5
NS = 5
ET = 16
LOADS = 3 + 3 * HG
C_B1, C_B2, C_W2, C_BB2, C_W3, C_BB3 = 0, 4, 5, 6, 7, 8
NCOL = 9

STEP = {
    "row_weights": (9, 10, 13, 22, 25, 27, 33, 38, 39, 47, 50, 50, 58, 60, 64, 66),
    "invert_sums": (8, 9, 13, 22, 25, 27, 31, 35, 39, 41, 49, 49, 57, 57, 62, 66),
    "sum_heads": (17, 19, 25, 27, 30, 32, 39, 41, 48, 51, 52, 56, 61, 64, 74, 77),
    "exp_mean": (25, 43, 56, 75),
    "transpose_mean": (43, 54, 65, 84),
    "relative": (43, 54, 66, 84),
    "attend": (46, 57, 79, 88),
    "invert_row": (51, 60, 78, 87),
    "residual": (51, 61, 79, 89),
    "stats0": (56, 62, 86, 90),
    "spread": (91, 106, 141),
    "power": (92, 110, 142),
    "apply0": (93, 95),
    "norm1_weight": (98,),
    "norm1_bias": (100,),
    "stats1": (103, 103, 104, 104),
    "apply1": (107, 112),
    "norm2_turn": (115,),
    "norm2_out": (113,),
    "add_b2": (125,),
    "up": (118, 123, 125, 126),
    "relu": (118, 121, 124, 125),
    "down": (130, 133, 136, 140),
    "stats2": (140, 140, 140, 140),
    "apply2": (144, 144, 145, 147),
    "norm3_turn": (149,),
    "norm3_out": (147,),
    "norm3_weight": (172,),
    "norm3_bias": (186,),
    "project": (171, 164),
    "queries": (176,),
    "keys": (167,),
    "split_q": (179, 180),
    "split_k": (189, 190),
}
LAST = {"weight": 20, "bias": 21, "add_x": 22, "stats": 27, "spread": 28, "power": 29, "apply": 32, "turn": 37, "keep": 36}


def build(nc, x, wqk, bqk, w1t, w2t, cols, rows, fw1, fw2, fh1, fh2, fw3, fcols, frow, gmat, sel, ident, out):
    f32, f32r = mybir.dt.float32, mybir.dt.float32r
    ALU, ACT, AX = mybir.AluOpType, mybir.ActivationFunctionType, mybir.AxisListType.X
    ctx = ExitStack()
    with ctx:
        def sb(name, shape, dt=f32):
            return ctx.enter_context(nc.sbuf_tensor(name, shape, dt))

        def sem(name):
            return ctx.enter_context(nc.semaphore(name))

        qk_dram = nc.dram_tensor("qk_split", [B, 4, P, S], f32, kind="Internal").ap()

        y_dram = nc.dram_tensor("y_kept", [B, P, NT, E], f32, kind="Internal").ap()

        hc = [sb(f"hc{i}", [P, NT, E + 1]) for i in range(2)]
        hs = sb("hs", [P, B, NT, E])
        ex = sb("ex", [P, ET, S])
        negmax = sb("negmax", [P, ET])
        zsum = sb("zsum", [P, ET])
        zinv = sb("zinv", [P, ET])
        rw = sb("rw", [P, ET, QS])
        ew = sb("ew", [P, 2, S])
        pt = sb("pt", [P, 2, NT, P])
        g_sb = sb("g_sb", [P, NT, NT, P])
        sel_sb = sb("sel_sb", [P, QS])
        id_sb = sb("id_sb", [P, P])
        z2inv = sb("z2inv", [P, NT])
        turn = sb("turn", [P, 1])
        one = sb("one", [P, 1])
        res = sb("res", [P, NT, E])
        bn = sb("bn", [P, 4, NT, 6])
        mv = sb("mv", [P, 4, NT, 2])
        veps = sb("veps", [P, 4, NT])
        rstd = sb("rstd", [P, 4, NT])
        nhalf = sb("nhalf", [P, NT])
        xh1 = sb("xh1", [P, NT, E])
        aff = sb("aff", [P, NT, E])
        out3 = sb("out3", [P, NT, E])
        xh2 = sb("xh2", [P, NT, E])
        h2t = sb("h2t", [P, S])
        h2r = sb("h2r", [P, S])
        relu = sb("relu", [P, CH, S])
        xh3 = sb("xh3", [P, NT, E])
        h3 = sb("h3", [P, NT, E])
        qf = sb("qf", [P, S])
        kf = sb("kf", [P, S])
        qhi, qlo = sb("qhi", [P, S], f32r), sb("qlo", [P, S], f32r)
        khi, klo = sb("khi", [P, S], f32r), sb("klo", [P, S], f32r)
        xin = [sb(f"xin{i}", [P, NT, E]) for i in range(2)]
        wqk_sb = sb("wqk_sb", [P, 2, E])
        bqk_sb = sb("bqk_sb", [P, 2])
        w1_sb = sb("w1_sb", [P, F])
        w2_sb = sb("w2_sb", [P, CH, E])
        col = sb("col", [P, NCOL])
        row = sb("row", [P, 2, E])
        row3 = sb("row3", [P, 2, E])
        att = ctx.enter_context(ExitStack())

        def att_sb(name, shape, dt=f32):
            return att.enter_context(nc.sbuf_tensor(name, shape, dt))

        qb = [att_sb(f"qb{i}", [96, NG, HG, S], f32r) for i in range(2)]
        kb = [att_sb(f"kb{i}", [96, NG, S], f32r) for i in range(2)]
        att.close()
        gate = [ex[:, CH * i:CH * i + CH, :] for i in range(2)]
        hid = [ex[:, CH * (2 + i):CH * (3 + i), :] for i in range(2)]
        hid_hi = [sb(f"hid_hi{i}", [P, CH, S], f32r) for i in range(2)]
        hid_lo = [sb(f"hid_lo{i}", [P, CH, S], f32r) for i in range(2)]
        fh_hi = [sb(f"fh_hi{i}", [P, CH, F], f32r) for i in range(2)]
        fh_lo = [sb(f"fh_lo{i}", [P, CH, F], f32r) for i in range(2)]
        fh_raw = [g_sb[:, :, :, :].rearrange("p i c l -> p (i c l)"), relu[:, :, :].rearrange("p c s -> p (c s)")]
        fw1_sb, fw2_sb = sb("fw1_sb", [P, F]), sb("fw2_sb", [P, F])
        fw3_sb = sb("fw3_sb", [P, CH, E])
        fcol = sb("fcol", [P, 4, CH])
        frow_sb = sb("frow_sb", [P, E])
        y_sb = [sb(f"y{i}", [P, NT, E]) for i in range(2)]

        sc = [ctx.enter_context(nc.psum_tensor(f"sc{i}", [P, S], f32)) for i in range(NS)]
        mean = ctx.enter_context(nc.psum_tensor("mean", [P, S], f32))
        m0 = ctx.enter_context(nc.psum_tensor("m0", [P, S], f32))
        m1 = ctx.enter_context(nc.psum_tensor("m1", [P, S], f32))
        up_bank = [m1, m1, m1, m0]
        banks = [*sc, mean, m0, m1]

        const_loaded = sem("const_loaded")
        ident_loaded = sem("ident_loaded")
        qkw_loaded = sem("qkw_loaded")
        filled = sem("filled")
        x_loaded = [sem(f"x_loaded{i}") for i in range(2)]
        row_loaded = sem("row_loaded")
        row3_loaded = sem("row3_loaded")
        layer_loaded = sem("layer_loaded")
        next_loaded = sem("next_loaded")
        net_loaded = sem("net_loaded")
        qk_loaded = [sem(f"qk_loaded{i}") for i in range(2)]
        hc_loaded = [sem(f"hc_loaded{i}") for i in range(2)]
        kept = sem("kept")
        scores_ready = sem("scores_ready")
        max_ready = sem("max_ready")
        exp_ready = sem("exp_ready")
        zinv_ready = sem("zinv_ready")
        weights_ready = sem("weights_ready")
        summed = sem("summed")
        ew_ready = sem("ew_ready")
        ewt_ready = sem("ewt_ready")
        pt_ready = sem("pt_ready")
        sa_ready = sem("sa_ready")
        z2_ready = sem("z2_ready")
        res_ready = sem("res_ready")
        bn_ready = [sem(f"bn_ready{i}") for i in range(4)]
        mv_ready = [sem(f"mv_ready{i}") for i in range(4)]
        veps_ready = [sem(f"veps_ready{i}") for i in range(4)]
        rstd_ready = [sem(f"rstd_ready{i}") for i in range(4)]
        centered = [sem(f"centered{i}") for i in range(2)]
        xh_ready = [sem(f"xh_ready{i}") for i in range(4)]
        h1a_ready, h1_ready = sem("h1a_ready"), sem("h1_ready")
        xh2t_ready = sem("xh2t_ready")
        h2t_ready, h2r_ready = sem("h2t_ready"), sem("h2r_ready")
        up_ready, relu_ready = sem("up_ready"), sem("relu_ready")
        down_ready = sem("down_ready")
        h3a_ready, h3_ready = sem("h3a_ready"), sem("h3_ready")
        xh3t_ready, ht_ready = sem("xh3t_ready"), sem("ht_ready")
        q_ready, k_ready = sem("q_ready"), sem("k_ready")
        qf_ready, kf_ready = sem("qf_ready"), sem("kf_ready")
        qhi_ready, khi_ready = sem("qhi_ready"), sem("khi_ready")
        split_ready = sem("split_ready")
        y_ready = sem("y_ready")
        raw_loaded = [sem(f"raw_loaded{i}") for i in range(2)]
        weights_high, weights_split = sem("weights_high"), sem("weights_split")
        g_high, g_split = sem("g_high"), sem("g_split")
        g_mm, g_silu, g_hid = sem("g_mm"), sem("g_silu"), sem("g_hid")
        g_a, g_b = sem("g_a"), sem("g_b")
        g_gelu = sem("g_gelu")
        g_out, g_scaled, g_done = sem("g_out"), sem("g_scaled"), sem("g_done")
        y_loaded = [sem(f"y_loaded{i}") for i in range(2)]
        stored = sem("stored")

        def bank_user(j):
            if j >= NS:
                return j - NS
            last = [n for n in range(TILES) if n % NS == j][-1]
            return last - TILES

        def permuted(q):
            return q[:, :].rearrange("p (k i n) -> p i n k", i=NT, n=4)

        def by_tile(q):
            return q[:, :].rearrange("p (i n k) -> p i n k", i=NT, n=4)

        def wait_later(engine, what, count):
            if type(count) is not int or count > 0:
                engine.wait_ge(what, count)

        def due(step, i, j, turn):
            lag, at = divmod(STEP[step][i], TILES)
            return [turn[lag]] if at == j and turn[lag] is not None else []

        def turn_of(u, par, scores, tail, late):
            return ((u + 1, 1 - par) if scores else None, (u, par) if tail else None, (u - 1, 1 - par) if late else None)

        def turns(fori, body):
            body(-1, 1, -1, scores=True, tail=False, late=None)
            body(0, 0, 0, scores=True, tail=True, late=None)
            body(1, 1, 0, scores=True, tail=True, late="inner")
            with fori(1, (U - B) // 2) as v:
                for par in range(2):
                    body(v * 2 + par, par, v, scores=True, tail=True, late="inner")
            v = (U - B) // 2
            body(U - B, 0, v, scores=True, tail=True, late="inner")
            body(U - B + 1, 1, v, scores=True, tail=True, late="last")
            with fori(v + 1, U // 2 - 1) as v:
                for par in range(2):
                    body(v * 2 + par, par, v, scores=True, tail=True, late="last")
            body(U - 2, 0, U // 2 - 1, scores=True, tail=True, late="last")
            body(U - 1, 1, U // 2 - 1, scores=False, tail=True, late="last")
            body(U, 0, U // 2, scores=False, tail=False, late="last")

        block = ctx.enter_context(nc.Block())

        @block.sync
        def _(sp):
            def load_x(b, n, par):
                sp.dma_start(xin[par][:, :, :], x[bass.ds(b, 1), :, :, :].rearrange("a p t e -> p (a t) e")) \
                    .then_inc(x_loaded[par], 16)

            def store_split(b):
                for n, part in enumerate((qhi, qlo, khi, klo)):
                    sp.dma_start(qk_dram[bass.ds(b, 1), n, :, :].rearrange("a p s -> (a p) s"),
                                 part[:, :].bitcast(f32)).then_inc(kept, 16)

            def load_split(b, par):
                for part, src in enumerate((2, 3, 2)):
                    sp.dma_start(kb[par][32 * part:32 * part + 32, :, :].bitcast(f32),
                                 qk_dram[bass.ds(b, 1), src, :, :].rearrange("a (g r) s -> r (a g) s", g=NG)) \
                        .then_inc(qk_loaded[par], 16)
                for part, src in enumerate((0, 0, 1)):
                    for h in range(HG):
                        r = 32 * part + DH * h
                        sp.dma_start(qb[par][r:r + DH, :, h, :].bitcast(f32),
                                     qk_dram[bass.ds(b, 1), src, :, :]
                                     .rearrange("a (g h r) s -> h r (a g) s", g=NG, h=HG)[h]) \
                            .then_inc(qk_loaded[par], 16)

            def load_tokens(b, par):
                sp.dma_start(hc[par][:, :, 0:E], hs[:, bass.ds(b, 1), :, :].rearrange("p a t e -> p (a t) e")) \
                    .then_inc(hc_loaded[par], 16)

            def first_sequence(b, par):
                sp.wait_ge(xh_ready[3], b * NT + NT)
                load_x((b + 2) % B, 0, par)
                sp.wait_ge(split_ready, b * 2 + 2)
                store_split(b)

            load_x(0, 0, 0)
            sp.dma_start(wqk_sb[:, :, :], wqk[0]).then_inc(qkw_loaded, 16)
            sp.dma_start(bqk_sb[:, :], bqk[0]).then_inc(qkw_loaded, 16)
            sp.dma_start(id_sb[:, :], ident).then_inc(ident_loaded, 16)
            load_x(1, 0, 1)
            sp.dma_start(sel_sb[:, :], sel).then_inc(const_loaded, 16)
            sp.dma_start(g_sb[:, :, :, :], gmat).then_inc(const_loaded, 16)
            first_sequence(0, 0)
            first_sequence(1, 1)
            first_sequence(2, 0)
            first_sequence(3, 1)
            sp.wait_ge(filled, 3 + NG)
            sp.wait_ge(kept, 64 * NG)
            load_split(0, 0)
            with sp.Fori(2, B // 2) as v:
                for par in range(2):
                    first_sequence(v * 2 + par, par)
            sp.wait_ge(filled, 3 + B)
            sp.wait_ge(kept, 64 * B)
            load_split(1, 1)
            sp.wait_ge(h3_ready, B)
            load_tokens(0, 0)
            load_tokens(1, 1)

            def load_rows(n, first):
                one = bass.ds(n, 1)
                if not first:
                    sp.wait_ge(h1_ready, n * B)
                sp.dma_start(row[:, :, :], rows[one, 0:2, :].to_broadcast([P, 2, E])).then_inc(row_loaded, 16)

            def load_layer(n, first=False):
                one = bass.ds(n, 1)
                if not first:
                    sp.wait_ge(ht_ready, n * B + B)
                sp.dma_start(w1_sb[:, :], w1t[one, :, :].rearrange("a p f -> p (a f)")).then_inc(layer_loaded, 16)
                sp.dma_start(w2_sb[:, :, :], w2t[one, :, :, :].rearrange("a p c e -> p (a c) e")).then_inc(layer_loaded, 16)
                sp.dma_start(col[:, :], cols[one, :, :].rearrange("a p c -> p (a c)")).then_inc(layer_loaded, 16)
                if not first:
                    sp.wait_ge(h3_ready, n * B + B)
                sp.dma_start(row3[:, :, :], rows[one, 2:4, :].to_broadcast([P, 2, E])).then_inc(row3_loaded, 16)

            def load_next(n):
                sp.wait_ge(kf_ready, n * B + B)
                sp.wait_ge(qf_ready, n * B + B)
                nxt = bass.ds(n + 1, 1)
                sp.dma_start(wqk_sb[:, :, :], wqk[nxt, :, :, :].rearrange("a p c e -> p (a c) e")).then_inc(next_loaded, 16)
                sp.dma_start(bqk_sb[:, :], bqk[nxt, :, :].rearrange("a p c -> p (a c)")).then_inc(next_loaded, 16)

            def load_x_again(u, par):
                sp.dma_start(xin[par][:, :, :], x[bass.ds(u % B, 1), :, :, :].rearrange("a p t e -> p (a t) e")) \
                    .then_inc(x_loaded[par], 16)

            def body(u, par, late, layer=None, more=True, again=True):
                w = u - 1
                if layer is not None:
                    load_rows(layer, False)
                if more:
                    sp.wait_ge(scores_ready, u * TILES + TILES)
                    load_split((u + 2) % B, par)
                    sp.wait_ge(res_ready, u * NT + NT)
                    load_tokens((u + 2) % B, par)
                if layer is not None:
                    load_layer(layer)
                if late == "inner":
                    sp.wait_ge(split_ready, w * 2 + 2 * B + 2)
                    store_split(w % B)
                if late == "last":
                    sp.wait_ge(y_ready, w - (U - B) + 1)
                    sp.dma_start(y_dram[bass.ds(w % B, 1), :, :, :].rearrange("a p t e -> p (a t) e"), h3[:, :, :]) \
                        .then_inc(kept, 16)
                    if again:
                        load_x_again(w + 2, 1 - par)

            load_rows(0, True)
            load_layer(0, True)
            load_next(0)
            body(0, 0, None)
            body(1, 1, "inner")
            with sp.Fori(1, B // 2) as v:
                for par in range(2):
                    body(v * 2 + par, par, "inner")
            with sp.Fori(1, D - 1) as n:
                body(n * B, 0, "inner", layer=n)
                load_next(n)
                body(n * B + 1, 1, "inner")
                with sp.Fori(1, B // 2) as v:
                    for par in range(2):
                        body(n * B + v * 2 + par, par, "inner")
            body(U - B, 0, "inner", layer=D - 1)
            sp.wait_ge(kept, U * 64)
            body(U - B + 1, 1, "last")
            with sp.Fori(1, B // 2 - 1) as v:
                for par in range(2):
                    body(v * 2 + (U - B) + par, par, "last")
            sp.wait_ge(scores_ready, U * TILES)
            for dst, src in ((fw1_sb[:, :], fw1), (fw2_sb[:, :], fw2), (fw3_sb[:, :, :], fw3), (fcol[:, :, :], fcols), (frow_sb[:, :], frow.to_broadcast([P, E]))):
                sp.dma_start(dst, src).then_inc(net_loaded, 16)
            body(U - 2, 0, "last", more=False)
            sp.wait_ge(pt_ready, U * NT)
            sp.dma_start(fh_raw[0], fh1.rearrange("p k f -> p (k f)")).then_inc(raw_loaded[0], 16)
            body(U - 1, 1, "last", more=False, again=False)
            sp.wait_ge(down_ready, U * NT)
            sp.dma_start(fh_raw[1], fh2.rearrange("p k f -> p (k f)")).then_inc(raw_loaded[1], 16)
            body(U, 0, "last", more=False, again=False)

            def load_y(b, par):
                sp.dma_start(y_sb[par][:, :, :], y_dram[bass.ds(b, 1), :, :, :].rearrange("a p t e -> p (a t) e")) \
                    .then_inc(y_loaded[par], 16)

            sp.wait_ge(kept, 64 * U + 16 * B)
            load_y(0, 0)
            load_y(1, 1)
            def net_pair(v):
                for par in range(2):
                    b = v * 2 + par
                    sp.wait_ge(g_done, b + 1)
                    sp.dma_start(out[bass.ds(b, 1), :, :, :].rearrange("a p t e -> p (a t) e"), y_sb[par][:, :, :]) \
                        .then_inc(stored, 16)
                    sp.wait_ge(stored, b * 16 + 16)
                    load_y((b + 2) % B, par)

            net_pair(0)
            with sp.Fori(1, B // 2) as v:
                net_pair(v)
            for par in range(2):
                sp.wait_ge(y_loaded[par], 16 * (B // 2 + 1))

        @block.gpsimd
        def _(gp):
            gp.memset(one[:, :], 1.0)
            gp.memset(nhalf[:, :], -0.5).then_inc(filled, 1)
            for i in range(2):
                gp.memset(hc[i][:, :, E:E + 1], 1.0).then_inc(filled, 1)
            gp.wait_ge(filled, 3)

            def power(k, n):
                gp.wait_ge(veps_ready[k], n)
                nc.gpsimd.tensor_tensor(rstd[:, k, :], veps[:, k, :], nhalf[:, :], ALU.pow).then_inc(rstd_ready[k], 1)

            def low_part(full, high, low, full_ready, high_ready, n):
                gp.wait_ge(full_ready, n)
                nc.gpsimd.tensor_tensor(high[:, :], full[:, :], one[:, 0:1].to_broadcast([P, S]), ALU.mult) \
                    .then_inc(high_ready, 1)
                gp.wait_ge(high_ready, n)
                nc.gpsimd.tensor_tensor(low[:, :], full[:, :], high[:, :].bitcast(f32), ALU.subtract) \
                    .then_inc(split_ready, 1)

            def first_pair(v):
                for par in range(2):
                    b = v * 2 + par
                    power(3, b + 1)
                    gp.wait_ge(xh_ready[3], b * NT + NT)
                    nc.gpsimd.tensor_copy(hs[:, bass.ds(b, 1), :, :].rearrange("p a t e -> p (a t e)"),
                                          xh3[:, :, :].rearrange("p t e -> p (t e)")).then_inc(h3_ready, 1)
                    gp.memset(qb[b // NG][:, b % NG, :, :].bitcast(f32), 0.0).then_inc(filled, 1)

            for v in range(B // 2):
                first_pair(v)

            def row_weights(t, q):
                gp.wait_ge(zinv_ready, t * NQ + q + 1)
                c = 4 * q % ET
                nc.gpsimd.tensor_tensor(rw[:, c:c + 4, :],
                                        sel_sb[:, :].rearrange("p (a q) -> p a q", a=1).to_broadcast([P, 4, QS]),
                                        zinv[:, c:c + 4].rearrange("p (a q) -> p a q", q=1).to_broadcast([P, 4, QS]),
                                        ALU.mult).then_inc(weights_ready, 1)

            def high_part(full, high, full_ready, high_ready, n):
                gp.wait_ge(full_ready, n)
                nc.gpsimd.tensor_tensor(high[:, :], full[:, :], one[:, 0:1].to_broadcast([P, S]), ALU.mult) \
                    .then_inc(high_ready, 1)

            def low_part(full, high, low, high_ready, n):
                gp.wait_ge(high_ready, n)
                nc.gpsimd.tensor_tensor(low[:, :], full[:, :], high[:, :].bitcast(f32), ALU.subtract) \
                    .then_inc(split_ready, 1)

            gp.wait_ge(const_loaded, 32)

            def split_weights(m):
                gp.wait_ge(raw_loaded[m], 16)
                for k in range(CH):
                    nc.gpsimd.tensor_tensor(fh_hi[m][:, k, :], fh_raw[m][:, k * F:k * F + F], one[:, 0:1].to_broadcast([P, F]),
                                            ALU.mult).then_inc(weights_high, 1)
                gp.wait_ge(weights_high, m * CH + CH)
                for k in range(CH):
                    nc.gpsimd.tensor_tensor(fh_lo[m][:, k, :], fh_raw[m][:, k * F:k * F + F], fh_hi[m][:, k, :].bitcast(f32),
                                            ALU.subtract).then_inc(weights_split, 1)

            def center(dst, src, k, n):
                gp.wait_ge(veps_ready[k], n)
                nc.gpsimd.tensor_tensor(dst[:, :, :], src[:, :, :], mv[:, k, :, 0:1].to_broadcast([P, NT, E]), ALU.subtract) \
                    .then_inc(centered[k], 1)

            def scale(dst, k, n):
                gp.wait_ge(centered[k], n)
                gp.wait_ge(rstd_ready[k], n)
                nc.gpsimd.tensor_tensor(dst[:, :, :], dst[:, :, :],
                                        rstd[:, k, :].rearrange("p (t a) -> p t a", a=1).to_broadcast([P, NT, E]),
                                        ALU.mult).then_inc(xh_ready[k], 1)

            def scale_out(w):
                gp.wait_ge(row3_loaded, (w // B) * 16 + 16)
                gp.wait_ge(xh_ready[2], w * NT + NT)
                nc.gpsimd.tensor_tensor(out3[:, :, :], xh3[:, :, :], row3[:, 0:1, :].to_broadcast([P, NT, E]), ALU.mult) \
                    .then_inc(h3a_ready, 1)

            def shift_out(w, last):
                gp.wait_ge(h3a_ready, w + 1)
                dst = out3[:, :, :] if last else hs[:, bass.ds(w % B, 1), :, :].rearrange("p a t e -> p (a t) e")
                nc.gpsimd.tensor_tensor(dst, out3[:, :, :], row3[:, 1:2, :].to_broadcast([P, NT, E]), ALU.add) \
                    .then_inc(h3_ready, 1)

            def add_x(w, y, par):
                gp.wait_ge(h3_ready, w + B + 1)
                gp.wait_ge(x_loaded[1 - par], (y // 2) * 16 + (B // 2 + 1) * 16)
                wait_later(gp, kept, y * 16 + 64 * U)
                nc.gpsimd.tensor_tensor(h3[:, :, :], out3[:, :, :], xin[1 - par][:, :, :], ALU.add).then_inc(y_ready, 1)

            def body(u, par, v, scores, tail, late):
                turn = turn_of(u, par, scores, tail, late)
                w, y = u - 1, u - 1 - (U - B)
                inner, last = late == "inner", late == "last"
                for j in range(TILES):
                    for q in range(NQ):
                        for n, side in due("row_weights", q, j, turn):
                            row_weights(n, q)
                    for n, side in due("power", 0, j, turn):
                        power(0, n + 1)
                    for n, side in due("apply0", 0, j, turn):
                        center(xh1, res, 0, n + 1)
                    for n, side in due("apply0", 1, j, turn):
                        scale(xh1, 0, n + 1)
                    for n, side in due("norm1_weight", 0, j, turn):
                        gp.wait_ge(row_loaded, (n // B) * 16 + 16)
                        gp.wait_ge(xh_ready[0], n + 1)
                        nc.gpsimd.tensor_tensor(aff[:, :, :], xh1[:, :, :], row[:, 0:1, :].to_broadcast([P, NT, E]), ALU.mult) \
                            .then_inc(h1a_ready, 1)
                    for n, side in due("norm1_bias", 0, j, turn):
                        gp.wait_ge(h1a_ready, n + 1)
                        nc.gpsimd.tensor_tensor(aff[:, :, :], aff[:, :, :], row[:, 1:2, :].to_broadcast([P, NT, E]), ALU.add) \
                            .then_inc(h1_ready, 1)
                    for n, side in due("power", 1, j, turn):
                        power(1, n + 1)
                    for n, side in due("apply1", 0, j, turn):
                        center(xh2, aff, 1, n + 1)
                    for n, side in due("apply1", 1, j, turn):
                        scale(xh2, 1, n + 1)
                    for n, side in due("add_b2", 0, j, turn):
                        gp.wait_ge(layer_loaded, (n // B) * 48 + 48)
                        gp.wait_ge(h2t_ready, n + 1)
                        nc.gpsimd.tensor_tensor(h2r[:, :], h2t[:, :], col[:, C_B2:C_B2 + 1].to_broadcast([P, S]), ALU.add) \
                            .then_inc(h2r_ready, 1)
                        if type(n) is int and n == U - 1:
                            split_weights(0)
                    for n, side in due("power", 2, j, turn):
                        power(2, n + 1)
                    if inner:
                        for n, side in due("norm3_weight", 0, j, turn):
                            scale_out(n)
                        for n, side in due("norm3_bias", 0, j, turn):
                            shift_out(n, False)
                        for n, side in due("split_q", 0, j, turn):
                            gp.wait_ge(kept, n * 64 + 64 * B)
                            high_part(qf, qhi, qf_ready, qhi_ready, n + B + 1)
                        for n, side in due("split_q", 1, j, turn):
                            low_part(qf, qhi, qlo, qhi_ready, n + B + 1)
                        for n, side in due("split_k", 0, j, turn):
                            high_part(kf, khi, kf_ready, khi_ready, n + B + 1)
                        for n, side in due("split_k", 1, j, turn):
                            low_part(kf, khi, klo, khi_ready, n + B + 1)
                    if last and j == LAST["weight"]:
                        scale_out(w)
                    if last and j == LAST["bias"]:
                        shift_out(w, True)
                    if last and j == LAST["add_x"]:
                        add_x(w, y, par)
                    if last and j == LAST["power"]:
                        power(3, y + B + 1)

            turns(gp.Fori, body)
            split_weights(1)

        @block.vector
        def _(dve):
            def split(full, high, low, full_ready, high_ready, n):
                dve.wait_ge(full_ready, n)
                nc.vector.tensor_copy(high[:, :], full[:, :]).then_inc(high_ready, 1)
                dve.wait_ge(high_ready, n)
                nc.vector.tensor_tensor(low[:, :], full[:, :], high[:, :].bitcast(f32), ALU.subtract) \
                    .then_inc(split_ready, 1)

            def stats(src, k, i, src_ready, n):
                dve.wait_ge(src_ready, n)
                nc.vector.bn_stats(bn[:, k, i, :], src).then_inc(bn_ready[k], 1)

            def spread(k, n):
                for i in range(NT):
                    ins = nc.vector.bn_aggr(mv[:, k, i, :], bn[:, k, i, :])
                ins.then_inc(mv_ready[k], 1)
                dve.wait_ge(mv_ready[k], n)
                nc.vector.tensor_scalar(veps[:, k, :], mv[:, k, :, 1], EPS, None, ALU.add).then_inc(veps_ready[k], 1)

            def apply(dst, src, k, i, n):
                dve.wait_ge(rstd_ready[k], n)
                nc.vector.tensor_scalar(dst[:, i, :], src, mv[:, k, i, 0:1], rstd[:, k, i:i + 1],
                                        ALU.subtract, ALU.mult).then_inc(xh_ready[k], 1)

            dve.wait_ge(qkw_loaded, 32)
            def measure(b, par, v):
                for i in range(NT):
                    stats(xin[par][:, i, :], 3, i, x_loaded[par], v * 16 + 16)
                dve.wait_ge(bn_ready[3], b * NT + NT)
                nc.vector.memset(turn[:, :], 0.0)
                spread(3, b + 1)

            def norm(b, par):
                wait_later(dve, h3_ready, b)
                wait_later(dve, xh3t_ready, b)
                for i in range(NT):
                    apply(xh3, xin[par][:, i, :], 3, i, b + 1)

            def first_sequence(b, par, v):
                dve.wait_ge(q_ready, b + 1)
                nc.vector.tensor_scalar(permuted(qf), by_tile(m0), bqk_sb[:, 0:1], DH ** -0.5, ALU.add, ALU.mult) \
                    .then_inc(qf_ready, 1)
                if type(b) is not int or b < B - 1:
                    norm(b + 1, 1 - par)
                wait_later(dve, kept, b * 64)
                split(qf, qhi, qlo, qf_ready, qhi_ready, b + 1)
                split(kf, khi, klo, kf_ready, khi_ready, b + 1)
                if type(b) is not int or b < B - 2:
                    measure(b + 2, par, v + 1)

            measure(0, 0, 0)
            norm(0, 0)
            measure(1, 1, 0)
            first_sequence(0, 0, 0)
            first_sequence(1, 1, 0)
            with dve.Fori(1, B // 2 - 1) as v:
                for par in range(2):
                    first_sequence(v * 2 + par, par, v)
            first_sequence(B - 2, 0, B // 2 - 1)
            first_sequence(B - 1, 1, B // 2 - 1)
            dve.wait_ge(const_loaded, 32)

            def score_max(t, j):
                dve.wait_ge(scores_ready, t * TILES + j + 1)
                nc.vector.tensor_reduce(negmax[:, j % ET:j % ET + 1], sc[j % NS][:, :], AX, ALU.max, negate=True) \
                    .then_inc(max_ready, 1)

            def invert_sums(t, q):
                dve.wait_ge(exp_ready, t * TILES + 4 * q + 4)
                c = 4 * q % ET
                nc.vector.reciprocal(zinv[:, c:c + 4], zsum[:, c:c + 4]).then_inc(zinv_ready, 1)

            def relative(t, i):
                dve.wait_ge(ewt_ready, t * NT + i + 1)
                nc.vector.tensor_tensor(pt[:, i % 2, :, :], m0[:, :].rearrange("p (c l) -> p c l", c=NT),
                                        g_sb[:, i, :, :], ALU.mult).then_inc(pt_ready, 1)

            def invert_row(t, i):
                dve.wait_ge(sa_ready, t * NT + i + 1)
                nc.vector.reciprocal(z2inv[:, i:i + 1], m0[:, E:E + 1]).then_inc(z2_ready, 1)

            def residual(t, i, par):
                dve.wait_ge(z2_ready, t * NT + i + 1)
                nc.vector.scalar_tensor_tensor(res[:, i, :], m0[:, 0:E], z2inv[:, i:i + 1],
                                               hc[par][:, i, 0:E], ALU.mult, ALU.add).then_inc(res_ready, 1)

            def split_hidden(par, c, n):
                nc.vector.tensor_copy(hid_hi[par][:, c, :], hid[par][:, c, :]).then_inc(g_high, 1)
                dve.wait_ge(g_high, n)
                nc.vector.tensor_tensor(hid_lo[par][:, c, :], hid[par][:, c, :], hid_hi[par][:, c, :].bitcast(f32),
                                        ALU.subtract).then_inc(g_split, 1)

            def net_first(v, par):
                b = v * 2 + par
                if type(v) is int:
                    dve.wait_ge(net_loaded, 5 * 16)
                for c in range(CH):
                    dve.wait_ge(g_silu, b * CH + c + 1)
                    nc.vector.scalar_tensor_tensor(hid[par][:, c, :], banks[4 + c % 2][:, :], fcol[:, 1, c:c + 1],
                                                   gate[par][:, c, :], ALU.mult, ALU.mult).then_inc(g_hid, 1)
                    dve.wait_ge(g_hid, b * CH + c + 1)
                    split_hidden(par, c, v * (4 * CH) + par * CH + c + 1)

            def net_rest(v):
                for par in range(2):
                    b = v * 2 + par
                    dve.wait_ge(g_a, b * CH + CH)
                    for c in range(CH):
                        dve.wait_ge(g_gelu, v * (4 * CH) + par * CH + c + 1)
                        split_hidden(par, c, v * (4 * CH) + (2 + par) * CH + c + 1)
                for par in range(2):
                    b = v * 2 + par
                    dve.wait_ge(g_out, b + 1)
                    nc.vector.tensor_tensor(gate[par][:, :, 0:E], banks[6 + par][:, :].rearrange("p (t e) -> p t e", t=NT),
                                            frow_sb[:, :].rearrange("p (a e) -> p a e", a=1).to_broadcast([P, NT, E]),
                                            ALU.mult).then_inc(g_scaled, 1)
                    dve.wait_ge(g_scaled, b + 1)
                    dve.wait_ge(y_loaded[par], v * 16 + 16)
                    nc.vector.tensor_tensor(y_sb[par][:, :, :], y_sb[par][:, :, :], gate[par][:, :, 0:E], ALU.add) \
                        .then_inc(g_done, 1)

            def body(u, par, v, scores, tail, late):
                turn = turn_of(u, par, scores, tail, late)
                y = u - 1 - (U - B) + B
                inner, last = late == "inner", late == "last"
                for j in range(TILES):
                    for k in range(3):
                        for n, side in due("spread", k, j, turn):
                            dve.wait_ge(bn_ready[k], n * NT + NT)
                    if last and j == LAST["spread"]:
                        dve.wait_ge(bn_ready[3], y * NT + NT)
                    if scores:
                        score_max(u + 1, j)
                    for q in range(NQ):
                        for n, side in due("invert_sums", q, j, turn):
                            invert_sums(n, q)
                    for i in range(NT):
                        for n, side in due("relative", i, j, turn):
                            relative(n, i)
                        for n, side in due("invert_row", i, j, turn):
                            invert_row(n, i)
                        for n, side in due("residual", i, j, turn):
                            residual(n, i, side)
                        for n, side in due("stats0", i, j, turn):
                            stats(res[:, i, :], 0, i, res_ready, n * NT + i + 1)
                    for n, side in due("spread", 0, j, turn):
                        spread(0, n + 1)
                    for i in range(NT):
                        for n, side in due("stats1", i, j, turn):
                            stats(aff[:, i, :], 1, i, h1_ready, n + 1)
                    for n, side in due("spread", 1, j, turn):
                        spread(1, n + 1)
                        if type(n) is int and n == U - 1:
                            net_first(0, 1)
                    for i in range(NT):
                        for n, side in due("stats2", i, j, turn):
                            stats(m1[:, i * E:i * E + E], 2, i, down_ready, n * NT + NT)
                    for n, side in due("spread", 2, j, turn):
                        spread(2, n + 1)
                    for i in range(NT):
                        for n, side in due("apply2", i, j, turn):
                            apply(xh3, m1[:, i * E:i * E + E], 2, i, n + 1)
                    if inner:
                        for n, side in due("queries", 0, j, turn):
                            dve.wait_ge(q_ready, n + B + 1)
                            dve.wait_ge(split_ready, n * 2 + 2 * B)
                            nc.vector.tensor_scalar(permuted(qf), by_tile(m1), bqk_sb[:, 0:1], DH ** -0.5,
                                                    ALU.add, ALU.mult).then_inc(qf_ready, 1)
                    if last and j == LAST["stats"]:
                        for i in range(NT):
                            stats(h3[:, i, :], 3, i, y_ready, y - B + 1)
                    if last and j == LAST["spread"]:
                        spread(3, y + 1)
                    if last and j == LAST["apply"]:
                        for i in range(NT):
                            apply(xh3, h3[:, i, :], 3, i, y + 1)
                        if type(u) is int and u == U - 1:
                            net_first(0, 0)

            turns(dve.Fori, body)
            net_rest(0)
            with dve.Fori(1, B // 2) as v:
                for par in range(2):
                    net_first(v, par)
                net_rest(v)

        @block.scalar
        def _(act):
            act.wait_ge(qkw_loaded, 32)
            def first_pair(v):
                for par in range(2):
                    b = v * 2 + par
                    act.wait_ge(xh3t_ready, b + 1)
                    nc.scalar.activation(h2t[:, :], m1[:, :], ACT.Copy).then_inc(ht_ready, 1)
                    act.wait_ge(k_ready, b + 1)
                    wait_later(act, split_ready, b * 2)
                    nc.scalar.activation(kf[:, :], mean[:, :], ACT.Identity, bias=bqk_sb[:, 1:2]).then_inc(kf_ready, 1)

            first_pair(0)
            with act.Fori(1, B // 2) as v:
                first_pair(v)

            def exp_scores(t, j):
                act.wait_ge(max_ready, t * TILES + j + 1)
                if j % 4 == 0 and (type(t) is not int or t > 0 or j >= ET):
                    act.wait_ge(summed, t * NQ + j // 4 - 3)
                c = j % ET
                nc.scalar.activation(ex[:, c, :], sc[j % NS][:, :], ACT.Exp, bias=negmax[:, c:c + 1],
                                     accum_out=zsum[:, c:c + 1]).then_inc(exp_ready, 1)

            def exp_mean(t, i):
                act.wait_ge(summed, t * NQ + 4 * i + 4)
                if type(t) is not int or t > 0 or i >= 2:
                    act.wait_ge(ewt_ready, t * NT + i - 1)
                nc.scalar.activation(ew[:, i % 2, :], mean[:, :], ACT.Exp).then_inc(ew_ready, 1)

            def affine(src, k, done):
                nc.scalar.activation(h2t[:, :], src[:, :], ACT.Identity, scale=col[:, k:k + 1], bias=col[:, k + 1:k + 2]) \
                    .then_inc(done, 1)

            def net_silu(v, par):
                b = v * 2 + par
                if type(v) is int:
                    act.wait_ge(net_loaded, 5 * 16)
                for c in range(CH):
                    act.wait_ge(g_mm, b * 2 * CH + 2 * c + 2)
                    wait_later(act, g_done, v * 2)
                    nc.scalar.activation(gate[par][:, c, :], banks[2 + c % 2][:, :], ACT.Silu,
                                         scale=fcol[:, 0, c:c + 1]).then_inc(g_silu, 1)

            def net_gelu(v, stage, par):
                b = v * 2 + par
                for c in range(CH):
                    act.wait_ge((g_a, g_b)[stage], b * CH + c + 1)
                    nc.scalar.activation(hid[par][:, c, :], banks[c % 2][:, :], ACT.Gelu,
                                         scale=fcol[:, 2 + stage, c:c + 1]).then_inc(g_gelu, 1)

            def body(u, par, v, scores, tail, late):
                turn = turn_of(u, par, scores, tail, late)
                w = u - 1
                inner, last = late == "inner", late == "last"
                for j in range(TILES):
                    if scores:
                        exp_scores(u + 1, j)
                    for i in range(NT):
                        for n, side in due("exp_mean", i, j, turn):
                            exp_mean(n, i)
                            if type(n) is int and n * NT + i == U * NT - 1:
                                net_silu(0, 0)
                    for n, side in due("norm2_out", 0, j, turn):
                        act.wait_ge(layer_loaded, (n // B) * 48 + 48)
                        act.wait_ge(xh2t_ready, n + 1)
                        affine(m1, C_W2, h2t_ready)
                    for c in range(CH):
                        for n, side in due("relu", c, j, turn):
                            act.wait_ge(up_ready, n * CH + c + 1)
                            nc.scalar.activation(relu[:, c, :], up_bank[c][:, :], ACT.Relu,
                                                 bias=col[:, C_B1 + c:C_B1 + c + 1]).then_inc(relu_ready, 1)
                            if type(n) is int and n * CH + c == U * CH - 1:
                                for side in range(2):
                                    net_gelu(0, 0, side)
                    if inner:
                        for n, side in due("norm3_out", 0, j, turn):
                            act.wait_ge(xh3t_ready, n + B + 1)
                            affine(m1, C_W3, ht_ready)
                        for n, side in due("keys", 0, j, turn):
                            act.wait_ge(k_ready, n + B + 1)
                            act.wait_ge(split_ready, n * 2 + 2 * B)
                            nc.scalar.activation(kf[:, :], m0[:, :], ACT.Identity, bias=bqk_sb[:, 1:2]).then_inc(kf_ready, 1)
                    if last and j == LAST["keep"]:
                        act.wait_ge(xh3t_ready, w - (U - B) + U + 1)
                        nc.scalar.activation(hs[:, bass.ds(w % B, 1), :, :].rearrange("p a t e -> p (a t) e"), m1[:, :],
                                             ACT.Copy).then_inc(ht_ready, 1)
                        if type(u) is int and u == U - 1:
                            net_silu(0, 1)

            turns(act.Fori, body)
            for par in range(2):
                net_gelu(0, 1, par)
            with act.Fori(1, B // 2) as v:
                for par in range(2):
                    net_silu(v, par)
                for stage in range(2):
                    for par in range(2):
                        net_gelu(v, stage, par)

        @block.tensor
        def _(pe):
            pe.wait_ge(ident_loaded, 16)
            pe.wait_ge(qkw_loaded, 32)
            def first_pair(v):
                for par in range(2):
                    b = v * 2 + par
                    pe.wait_ge(xh_ready[3], b * NT + NT)
                    for i in range(NT):
                        ins = nc.tensor.transpose(m1[:, i * P:i * P + P], xh3[:, i, :], id_sb[:, :])
                    ins.then_inc(xh3t_ready, 1)
                    pe.wait_ge(ht_ready, b + 1)
                    wait_later(pe, qf_ready, b)
                    nc.tensor.matmul(m0[:, :], wqk_sb[:, 0, :], h2t[:, :], start=True, stop=True).then_inc(q_ready, 1)
                    wait_later(pe, kf_ready, b)
                    nc.tensor.matmul(mean[:, :], wqk_sb[:, 1, :], h2t[:, :], start=True, stop=True).then_inc(k_ready, 1)

            first_pair(0)
            with pe.Fori(1, B // 2) as v:
                first_pair(v)

            def score_tile(t, j, par):
                q, n = j // 4, j % 4
                i, g = q // NG, q % NG
                free = bank_user(j)
                if type(t) is not int or t > 0 or free >= 0:
                    pe.wait_ge(exp_ready, t * TILES + free + 1)
                flat = qb[par][:, g, :, :].rearrange("r h s -> r (h s)")
                nc.tensor.matmul(sc[j % NS][:, :], flat[:, NT * i + n::S // QS], kb[par][:, g, :], start=True, stop=True) \
                    .then_inc(scores_ready, 1)

            def sum_heads(t, q):
                pe.wait_ge(weights_ready, t * NQ + q + 1)
                i, g = q // NG, q % NG
                if g == 0 and (type(t) is not int or t > 0 or i > 0):
                    pe.wait_ge(ew_ready, t * NT + i)
                for n in range(4):
                    c = (4 * q + n) % ET
                    ins = nc.tensor.matmul(mean[n * QS:(n + 1) * QS, :], rw[:, c, :], ex[:, c, :],
                                           start=(g == 0), stop=(g == NG - 1))
                ins.then_inc(summed, 1)

            def transpose_mean(t, i):
                pe.wait_ge(ew_ready, t * NT + i + 1)
                for c in range(NT):
                    ins = nc.tensor.transpose(m0[:, c * P:c * P + P], ew[:, i % 2, c * P:c * P + P], id_sb[:, :])
                ins.then_inc(ewt_ready, 1)

            def attend(t, i, par, loaded):
                pe.wait_ge(hc_loaded[par], loaded)
                pe.wait_ge(pt_ready, t * NT + i + 1)
                for c in range(NT):
                    ins = nc.tensor.matmul(m0[:, 0:E + 1], pt[:, i % 2, c, :], hc[par][:, c, :],
                                           start=(c == 0), stop=(c == NT - 1))
                ins.then_inc(sa_ready, 1)

            def transpose_tokens(src, done):
                for i in range(NT):
                    ins = nc.tensor.transpose(m1[:, i * P:i * P + P], src[:, i, :], id_sb[:, :])
                ins.then_inc(done, 1)

            def up(c):
                nc.tensor.matmul(up_bank[c][:, :], w1_sb[:, c * P:c * P + P], h2t[:, :], start=True, stop=True) \
                    .then_inc(up_ready, 1)

            def down(i):
                dst = m1[:, i * E:i * E + E]
                nc.tensor.matmul(dst, h2r[:, i * P:i * P + P], id_sb[:, :], start=True, stop=False)
                for c in range(CH):
                    ins = nc.tensor.matmul(dst, relu[:, c, i * P:i * P + P], w2_sb[:, c, :], start=False, stop=(c == CH - 1))
                ins.then_inc(down_ready, 1)

            def net_first(v, par):
                b = v * 2 + par
                if type(v) is int:
                    pe.wait_ge(net_loaded, 5 * 16)
                    pe.wait_ge(ht_ready, U + b + 1)
                yt = hs[:, bass.ds(b, 1), :, :].rearrange("p a t e -> p (a t e)")
                for c in range(CH):
                    wait_later(pe, g_hid, v * (2 * CH) + max(par * CH + c - 1, 0))
                    nc.tensor.matmul(banks[2 + c % 2][:, :], fw1_sb[:, c * P:c * P + P], yt, start=True, stop=True) \
                        .then_inc(g_mm, 1)
                    nc.tensor.matmul(banks[4 + c % 2][:, :], fw2_sb[:, c * P:c * P + P], yt, start=True, stop=True) \
                        .then_inc(g_mm, 1)

            def net_square(v, stage, par):
                if type(v) is int:
                    pe.wait_ge(weights_split, stage * CH + CH)
                pe.wait_ge(g_split, v * (4 * CH) + (2 * stage + par) * CH + CH)
                for c in range(CH):
                    wait_later(pe, g_gelu, v * (4 * CH) + max(stage * 2 * CH + par * CH + c - 1, 0))
                    cols_c = slice(c * P, c * P + P)
                    for k in range(CH):
                        for n, (w, h) in enumerate(((fh_hi, hid_hi), (fh_hi, hid_lo), (fh_lo, hid_hi))):
                            ins = nc.tensor.matmul(banks[c % 2][:, :], w[stage][:, k, cols_c], h[par][:, k, :],
                                                   start=(k == 0 and n == 0), stop=(k == CH - 1 and n == 2))
                    ins.then_inc((g_a, g_b)[stage], 1)

            def net_out(v, par):
                pe.wait_ge(g_gelu, v * (4 * CH) + (3 + par) * CH)
                wait_later(pe, g_scaled, v * 2)
                for i in range(NT):
                    for k in range(CH):
                        ins = nc.tensor.matmul(banks[6 + par][:, i * E:i * E + E], hid[par][:, k, i * P:i * P + P],
                                               fw3_sb[:, k, :], start=(k == 0), stop=(k == CH - 1))
                ins.then_inc(g_out, 1)

            def body(u, par, v, scores, tail, late):
                turn = turn_of(u, par, scores, tail, late)
                t, tp, w = u + 1, 1 - par, u - 1
                tv = v + par
                inner, last = late == "inner", late == "last"
                for j in range(TILES):
                    if scores:
                        if j == 0:
                            pe.wait_ge(qk_loaded[tp], tv * (16 * LOADS) + 16 * LOADS)
                        score_tile(t, j, tp)
                    for q in range(NQ):
                        for n, side in due("sum_heads", q, j, turn):
                            sum_heads(n, q)
                    for i in range(NT):
                        for n, side in due("transpose_mean", i, j, turn):
                            if i == 0 and inner:
                                pe.wait_ge(kf_ready, w + B + 1)
                            if i == 2 and (type(n) is not int or n > 0):
                                pe.wait_ge(relu_ready, n * CH)
                            if type(n) is not int or n * NT + i > 0:
                                pe.wait_ge(res_ready, n * NT + i)
                            transpose_mean(n, i)
                        for n, side in due("attend", i, j, turn):
                            attend(n, i, side, (n // 2) * 16 + 16)
                            if type(n) is int and n * NT + i == U * NT - 1:
                                net_first(0, 0)
                    for n, side in due("norm2_turn", 0, j, turn):
                        if inner:
                            pe.wait_ge(qf_ready, n + B)
                        if last:
                            pe.wait_ge(ht_ready, n + B)
                        pe.wait_ge(xh_ready[1], n + 1)
                        transpose_tokens(xh2, xh2t_ready)
                    for c in range(CH):
                        for n, side in due("up", c, j, turn):
                            if c == 0:
                                pe.wait_ge(layer_loaded, (n // B) * 48 + 48)
                                pe.wait_ge(h2t_ready, n + 1)
                            if c in (1, 2):
                                pe.wait_ge(relu_ready, n * CH + c)
                            if c == 3 and scores:
                                pe.wait_ge(res_ready, t * NT + 2)
                            if c == 3 and not scores:
                                pe.wait_ge(res_ready, n * NT + 4)
                            up(c)
                    for i in range(NT):
                        for n, side in due("down", i, j, turn):
                            if i == 0:
                                pe.wait_ge(relu_ready, n * CH + 4)
                                pe.wait_ge(h2r_ready, n + 1)
                            down(i)
                            if type(n) is int and n * NT + i == U * NT - 1:
                                for side in range(2):
                                    net_square(0, 0, side)
                    if inner:
                        for n, side in due("norm3_turn", 0, j, turn):
                            pe.wait_ge(xh_ready[2], n * NT + NT)
                            transpose_tokens(xh3, xh3t_ready)
                        for n, side in due("project", 0, j, turn):
                            pe.wait_ge(ht_ready, n + B + 1)
                            pe.wait_ge(next_loaded, (n // B) * 32 + 32)
                            nc.tensor.matmul(m1[:, :], wqk_sb[:, 0, :], h2t[:, :], start=True, stop=True).then_inc(q_ready, 1)
                        for n, side in due("project", 1, j, turn):
                            pe.wait_ge(ht_ready, n + B + 1)
                            pe.wait_ge(next_loaded, (n // B) * 32 + 32)
                            pe.wait_ge(res_ready, n * NT + 2 * NT)
                            nc.tensor.matmul(m0[:, :], wqk_sb[:, 1, :], h2t[:, :], start=True, stop=True).then_inc(k_ready, 1)
                    if last and j == LAST["turn"]:
                        pe.wait_ge(xh_ready[3], (w - (U - B) + B) * NT + NT)
                        transpose_tokens(xh3, xh3t_ready)
                        if type(u) is int and u == U - 1:
                            net_first(0, 1)

            turns(pe.Fori, body)
            pe.wait_ge(res_ready, U * NT)
            pe.wait_ge(ht_ready, U + B)
            for par in range(2):
                net_square(0, 1, par)
            for par in range(2):
                net_out(0, par)
            with pe.Fori(1, B // 2) as v:
                for par in range(2):
                    net_first(v, par)
                for stage in range(2):
                    for par in range(2):
                        net_square(v, stage, par)
                for par in range(2):
                    net_out(v, par)


def kernel(**inputs):
    import numpy as np
    import concourse.bacc as bacc
    from concourse.bass_utils import run_bass_kernel_spmd

    a = {k.removeprefix("L0_"): np.asarray(v) for k, v in inputs.items()}

    def tokens(z):
        return z.reshape(B, NT, P, E).transpose(0, 2, 1, 3)

    def chunks(w):
        return w.T.reshape(-1, P, w.shape[0]).transpose(1, 0, 2)

    def split_col(v):
        return v.reshape(-1, P).T

    wqk = np.stack([a["attn_Wq"].transpose(0, 2, 1), a["attn_Wk"].transpose(0, 2, 1)], axis=2)
    bqk = np.stack([a["attn_bq"], a["attn_bk"]], axis=2)
    cols = np.stack([np.concatenate([split_col(a["attn_b1"][n]), a["attn_b2"][n][:, None],
                                     a["attn_ln2_w"][n][:, None], a["attn_ln2_b"][n][:, None],
                                     a["attn_ln3_w"][n][:, None], a["attn_ln3_b"][n][:, None]], axis=1) for n in range(D)])
    rows = np.stack([a["attn_ln1_w"], a["attn_ln1_b"], a["attn_ln3_w"], a["attn_ln3_b"]], axis=1)
    pos = np.arange(S)
    rel = np.exp(-np.abs(pos[:, None] - pos[None, :]).astype(np.float64) / 16.0)
    gmat = np.exp(rel).astype(np.float32).reshape(NT, P, NT, P).transpose(3, 0, 2, 1)
    sel = np.tile(np.eye(QS, dtype=np.float32) / H, (HG, 1))
    arrays = {
        "x": tokens(a["attn_x"]), "wqk": wqk, "bqk": bqk,
        "w1t": a["attn_W1"].transpose(0, 2, 1),
        "w2t": np.stack([chunks(a["attn_W2"][n]) for n in range(D)]),
        "cols": cols, "rows": rows,
        "fw1": a["ffn_w1_w"].T, "fw2": a["ffn_w2_w"].T, "fh1": chunks(a["ffn_h1_w"]), "fh2": chunks(a["ffn_h2_w"]),
        "fw3": chunks(a["ffn_w3_w"]),
        "fcols": np.stack([split_col(a[f"ffn_{n}_s"]) for n in ("w1", "w2", "h1", "h2")], axis=1),
        "frow": a["ffn_w3_s"][None, :],
        "gmat": gmat, "sel": sel, "ident": np.eye(P, dtype=np.float32),
    }
    arrays = {k: np.ascontiguousarray(v) for k, v in arrays.items()}
    nc = bacc.Bacc("TRN2", target_bir_lowering=False, num_devices=1)
    aps = [nc.dram_tensor(k, v.shape, mybir.dt.from_np(v.dtype), kind="ExternalInput").ap() for k, v in arrays.items()]
    out = nc.dram_tensor("out", (B, P, NT, E), mybir.dt.float32, kind="ExternalOutput").ap()
    build(nc, *aps, out)
    r = run_bass_kernel_spmd(nc, [arrays], core_ids=[0])
    return np.asarray(r.results[0]["out"]).reshape(B, P, NT, E).transpose(0, 2, 1, 3).reshape(B, S, E)
```
